# Optimizing a Trainium2 kernel written in Bass

```python
import numpy as np
import jax
import jax.numpy as jnp

def _softmax(x, axis=-1):
    return jax.nn.softmax(x, axis=axis)

def _gelu(x):
    return jax.nn.gelu(x, approximate=True)

def _silu(x):
    return jax.nn.silu(x)

def _sigmoid(x):
    return jax.nn.sigmoid(x)

def _layernorm(x, axis=-1, eps=1e-05):
    m = jnp.mean(x, axis=axis, keepdims=True)
    v = jnp.var(x, axis=axis, keepdims=True)
    return (x - m) / jnp.sqrt(v + eps)

def _scatter_add(tgt, idx, src, axis=0):
    return tgt.at[idx].add(src)

def _segment_sum(src, seg, n):
    return jax.ops.segment_sum(src, seg, n)
kernel_name = 'mk_adaln_attn_ffn_d1_seqx_r4_777dbb'

def setup_inputs(seed: int=0):
    np.random.seed(seed)
    _w = jnp.asarray

    def _rec_inputs():
        import jax
        import jax.numpy as jnp
        _rk = jax.random.key(seed)
        x = -0.000125 + 0.9999 * jax.random.normal(jax.random.fold_in(_rk, 1), (32, 64, 1024), jnp.float32)
        _lenS = 64 - jax.random.randint(jax.random.fold_in(_rk, 7), (32,), 0, max(1, 64 // 4) + 1, jnp.int32)
        _lenS2 = 64 - jax.random.randint(jax.random.fold_in(_rk, 8), (32,), 0, max(1, 64 // 4) + 1, jnp.int32)
        itok_B_0_23 = jax.random.randint(jax.random.fold_in(_rk, 11), (32,), 0, 24, jnp.int32)
        itok_B_0_7 = jax.random.randint(jax.random.fold_in(_rk, 12), (32,), 0, 8, jnp.int32)
        return (x, itok_B_0_23, itok_B_0_7)
    x, itok_B_0_23, itok_B_0_7 = _rec_inputs()

    def _L0_cond_setup():
        import jax, jax.numpy as jnp
        import numpy as np
        R = 16
        ALPHA = 32
        SCALING = ALPHA / R
        SLOTS = 32
        IN_F = 1024
        OUT_F = 1024
        B, T = (8, 256)
        key = jax.random.key(seed)
        k1, k2, k3, k4, k5, k6 = jax.random.split(key, 6)
        x = jax.random.normal(k1, (B, T, IN_F), dtype=jnp.float32)
        adapter_mapping = jax.random.randint(k2, (B,), 0, SLOTS, dtype=jnp.int32)
        W = jax.random.normal(k3, (OUT_F, IN_F), dtype=jnp.float32) * 0.02
        b = jax.random.normal(k4, (OUT_F,), dtype=jnp.float32) * 0.02
        lora_As = jax.random.normal(k5, (SLOTS, IN_F, R), dtype=jnp.float32) * 0.02
        lora_Bs = jax.random.normal(k6, (SLOTS, R, OUT_F), dtype=jnp.float32) * 0.02
        return {'x': x, 'adapter_mapping': adapter_mapping, 'W': W, 'b': b, 'lora_As': lora_As, 'lora_Bs': lora_Bs}
    _L0_cond_all = _L0_cond_setup()
    _L0_cond_in = {k: v for k, v in _L0_cond_all.items() if k in ('W', 'b', 'lora_As', 'lora_Bs')}
    del _L0_cond_all

    def _L0_attn_setup():
        import jax, jax.numpy as jnp
        import numpy as np
        HIDDEN = 1024
        HEAD_DIM = 128
        N_Q_HEADS = 32
        N_KV_HEADS = 8
        SLIDING_WINDOW = 256
        ROPE_THETA = 10000.0
        BATCH, SEQ = (1, 512)

        def _rope(t, pos):
            d = t.shape[-1]
            half = d // 2
            inv_freq = ROPE_THETA ** (-jnp.arange(half, dtype=jnp.float32) / half)
            ang = pos[:, None].astype(jnp.float32) * inv_freq[None, :]
            cos = jnp.cos(ang)[None, :, None, :]
            sin = jnp.sin(ang)[None, :, None, :]
            t1, t2 = (t[..., :half], t[..., half:])
            return jnp.concatenate([t1 * cos - t2 * sin, t1 * sin + t2 * cos], axis=-1)
        key = jax.random.key(seed)
        ks = jax.random.split(key, 5)
        w_scale = HIDDEN ** (-0.5)
        return {'x': jax.random.normal(ks[0], (BATCH, SEQ, HIDDEN), jnp.float32), 'wq': jax.random.normal(ks[1], (HIDDEN, N_Q_HEADS * HEAD_DIM), jnp.float32) * w_scale, 'wk': jax.random.normal(ks[2], (HIDDEN, N_KV_HEADS * HEAD_DIM), jnp.float32) * w_scale, 'wv': jax.random.normal(ks[3], (HIDDEN, N_KV_HEADS * HEAD_DIM), jnp.float32) * w_scale, 'wo': jax.random.normal(ks[4], (N_Q_HEADS * HEAD_DIM, HIDDEN), jnp.float32) * w_scale}
    _L0_attn_all = _L0_attn_setup()
    _L0_attn_in = {k: v for k, v in _L0_attn_all.items() if k in ('wq', 'wk', 'wv', 'wo')}
    del _L0_attn_all

    def _L0_cond2_setup():
        import jax, jax.numpy as jnp
        import numpy as np
        TOP_K = 2
        LANG_BIAS = 5.0
        SCALING = 32.0 / 16.0
        LANGUAGE_PAD_ID = -1
        key = jax.random.key(seed)
        ks = jax.random.split(key, 6)
        B, T, D, O, E, R = (4, 512, 1024, 1024, 8, 16)
        x = jax.random.normal(ks[0], (B, T, D), dtype=jnp.float32)
        language_ids = jax.random.randint(ks[1], (B,), 0, E).astype(jnp.int64)
        W = jax.random.normal(ks[2], (O, D), dtype=jnp.float32) * (1.0 / np.sqrt(D))
        Wr = jax.random.normal(ks[3], (E, D), dtype=jnp.float32) * (1.0 / np.sqrt(D))
        A = jax.random.normal(ks[4], (E, R, D), dtype=jnp.float32) * (1.0 / np.sqrt(D))
        Bm = jax.random.normal(ks[5], (O, R), dtype=jnp.float32) * 0.0
        Bm = jnp.broadcast_to(Bm, (E, O, R)) + jax.random.normal(ks[5], (E, O, R), dtype=jnp.float32) * 0.02
        return {'x': x, 'language_ids': language_ids, 'W': W, 'Wr': Wr, 'A': A, 'B': Bm}
    _L0_cond2_all = _L0_cond2_setup()
    _L0_cond2_in = {k: v for k, v in _L0_cond2_all.items() if k in ('W', 'Wr', 'A', 'B')}
    del _L0_cond2_all

    def _L0_ffn_setup():
        import jax, jax.numpy as jnp
        import numpy as np
        TOP_K = 2
        SCALING = 32.0 / 64.0
        key = jax.random.key(seed)
        ks = jax.random.split(key, 6)
        Bsz, S, Din, Dout, R, E = (4, 512, 1024, 1024, 64, 16)
        x = jax.random.normal(ks[0], (Bsz, S, Din), dtype=jnp.float32)
        base_w = jax.random.normal(ks[1], (Dout, Din), dtype=jnp.float32) * 0.02
        base_b = jax.random.normal(ks[2], (Dout,), dtype=jnp.float32) * 0.02
        A = jax.random.normal(ks[3], (R, Din), dtype=jnp.float32) * (1.0 / np.sqrt(Din))
        B = jax.random.normal(ks[4], (E, Dout, R), dtype=jnp.float32) * 0.02
        router_w = jax.random.normal(ks[5], (E, Din), dtype=jnp.float32) * 0.02
        return {'x': x, 'base_w': base_w, 'base_b': base_b, 'A': A, 'B': B, 'router_w': router_w}
    _L0_ffn_all = _L0_ffn_setup()
    _L0_ffn_in = {k: v for k, v in _L0_ffn_all.items() if k in ('base_w', 'base_b', 'A', 'B', 'router_w')}
    del _L0_ffn_all
    return {'x': x, 'itok_B_0_23': itok_B_0_23, 'itok_B_0_7': itok_B_0_7, 'L0_cond_W': _L0_cond_in['W'], 'L0_cond_b': _L0_cond_in['b'], 'L0_cond_lora_As': _L0_cond_in['lora_As'], 'L0_cond_lora_Bs': _L0_cond_in['lora_Bs'], 'L0_attn_wq': _L0_attn_in['wq'], 'L0_attn_wk': _L0_attn_in['wk'], 'L0_attn_wv': _L0_attn_in['wv'], 'L0_attn_wo': _L0_attn_in['wo'], 'L0_cond2_W': _L0_cond2_in['W'], 'L0_cond2_Wr': _L0_cond2_in['Wr'], 'L0_cond2_A': _L0_cond2_in['A'], 'L0_cond2_B': _L0_cond2_in['B'], 'L0_ffn_base_w': _L0_ffn_in['base_w'], 'L0_ffn_base_b': _L0_ffn_in['base_b'], 'L0_ffn_A': _L0_ffn_in['A'], 'L0_ffn_B': _L0_ffn_in['B'], 'L0_ffn_router_w': _L0_ffn_in['router_w']}

def reference(x, itok_B_0_23, itok_B_0_7, L0_cond_W, L0_cond_b, L0_cond_lora_As, L0_cond_lora_Bs, L0_attn_wq, L0_attn_wk, L0_attn_wv, L0_attn_wo, L0_cond2_W, L0_cond2_Wr, L0_cond2_A, L0_cond2_B, L0_ffn_base_w, L0_ffn_base_b, L0_ffn_A, L0_ffn_B, L0_ffn_router_w):
    import jax
    import jax.numpy as jnp

    def _L0_cond_ref(x, adapter_mapping, W, b, lora_As, lora_Bs):
        import jax, jax.numpy as jnp
        import numpy as np
        R = 16
        ALPHA = 32
        SCALING = ALPHA / R
        SLOTS = 32
        IN_F = 1024
        OUT_F = 1024
        B, T = (8, 256)
        base_out = jnp.einsum('bti,oi->bto', x, W) + b
        A = lora_As[adapter_mapping]
        Bm = lora_Bs[adapter_mapping]
        lora_h = jnp.einsum('bti,bir->btr', x, A)
        lora_out = jnp.einsum('btr,bro->bto', lora_h, Bm)
        return base_out + lora_out * SCALING

    def _L0_attn_ref(x, wq, wk, wv, wo):
        import jax, jax.numpy as jnp
        import numpy as np
        HIDDEN = 1024
        HEAD_DIM = 128
        N_Q_HEADS = 32
        N_KV_HEADS = 8
        SLIDING_WINDOW = 256
        ROPE_THETA = 10000.0
        BATCH, SEQ = (1, 512)

        def _rope(t, pos):
            d = t.shape[-1]
            half = d // 2
            inv_freq = ROPE_THETA ** (-jnp.arange(half, dtype=jnp.float32) / half)
            ang = pos[:, None].astype(jnp.float32) * inv_freq[None, :]
            cos = jnp.cos(ang)[None, :, None, :]
            sin = jnp.sin(ang)[None, :, None, :]
            t1, t2 = (t[..., :half], t[..., half:])
            return jnp.concatenate([t1 * cos - t2 * sin, t1 * sin + t2 * cos], axis=-1)
        B, S, _ = x.shape
        G = N_Q_HEADS // N_KV_HEADS
        sm_scale = HEAD_DIM ** (-0.5)
        q = (x @ wq).reshape(B, S, N_Q_HEADS, HEAD_DIM)
        k = (x @ wk).reshape(B, S, N_KV_HEADS, HEAD_DIM)
        v = (x @ wv).reshape(B, S, N_KV_HEADS, HEAD_DIM)
        pos = jnp.arange(S)
        q = _rope(q, pos)
        k = _rope(k, pos)
        qg = q.reshape(B, S, N_KV_HEADS, G, HEAD_DIM)
        scores = jnp.einsum('bqhgd,bshd->bhgqs', qg, k) * sm_scale
        i = pos[:, None]
        j = pos[None, :]
        allowed = (j <= i) & (j > i - SLIDING_WINDOW)
        neg = jnp.finfo(scores.dtype).min
        scores = jnp.where(allowed[None, None, None], scores, neg)
        attn = jax.nn.softmax(scores, axis=-1)
        out = jnp.einsum('bhgqs,bshd->bqhgd', attn, v).reshape(B, S, N_Q_HEADS * HEAD_DIM)
        return out @ wo

    def _L0_cond2_ref(x, language_ids, W, Wr, A, B):
        import jax, jax.numpy as jnp
        import numpy as np
        TOP_K = 2
        LANG_BIAS = 5.0
        SCALING = 32.0 / 16.0
        LANGUAGE_PAD_ID = -1
        base = jnp.einsum('btd,od->bto', x, W)
        E = Wr.shape[0]
        logits = jnp.einsum('btd,ed->bte', x.astype(jnp.float32), Wr.astype(jnp.float32))
        expert_targets = language_ids
        valid = expert_targets >= 0
        tgt = jnp.where(valid, expert_targets, 0)
        bias = jax.nn.one_hot(tgt, E, dtype=logits.dtype) * LANG_BIAS
        bias = jnp.where(valid[:, None], bias, 0.0)
        logits = logits + bias[:, None, :]
        topw, topi = jax.lax.top_k(logits, TOP_K)
        weights = jax.nn.softmax(topw, axis=-1)
        gates = jnp.sum(jax.nn.one_hot(topi, E, dtype=weights.dtype) * weights[..., None], axis=-2)
        gates = gates.astype(x.dtype)
        h = jnp.einsum('btd,erd->bter', x, A)
        lora_out = jnp.einsum('bter,bte,eor->bto', h, gates, B)
        return base + SCALING * lora_out

    def _L0_ffn_ref(x, base_w, base_b, A, B, router_w):
        import jax, jax.numpy as jnp
        import numpy as np
        TOP_K = 2
        SCALING = 32.0 / 64.0
        base_out = jnp.einsum('bsi,oi->bso', x, base_w) + base_b
        res_hidden = jnp.einsum('bsi,ri->bsr', x, A)
        logits = jnp.einsum('bsi,ei->bse', x, router_w)
        probs = jax.nn.softmax(logits, axis=-1)
        topw, topi = jax.lax.top_k(probs, TOP_K)
        topw = topw / (jnp.sum(topw, axis=-1, keepdims=True) + 1e-06)
        num_experts = B.shape[0]
        combine = jnp.sum(jax.nn.one_hot(topi, num_experts, dtype=x.dtype) * topw[..., None], axis=-2)
        delta = jnp.einsum('bse,bsr,eor->bso', combine, res_hidden, B)
        return base_out + delta * SCALING
    x = x + _L0_attn_ref(_L0_cond_ref(x, itok_B_0_23, L0_cond_W, L0_cond_b, L0_cond_lora_As, L0_cond_lora_Bs), L0_attn_wq, L0_attn_wk, L0_attn_wv, L0_attn_wo)
    x = x + _L0_ffn_ref(_L0_cond2_ref(x, itok_B_0_7, L0_cond2_W, L0_cond2_Wr, L0_cond2_A, L0_cond2_B), L0_ffn_base_w, L0_ffn_base_b, L0_ffn_A, L0_ffn_B, L0_ffn_router_w)
    return x

_drawn_inputs = setup_inputs


def setup_inputs(seed=0):
    import zlib

    import numpy as np

    out = dict(_drawn_inputs(seed))
    spreads = {}
    factors = {'L0_cond2_Wr': 4.363, 'L0_ffn_base_b': 3.566}
    for name, (base, spread) in spreads.items():
        noise = np.random.default_rng([zlib.crc32(name.encode()), seed]).standard_normal(out[name].shape)
        drawn = base * np.exp(spread * noise) if base else spread * noise
        out[name] = jnp.asarray(drawn.astype(out[name].dtype))
    for name, factor in factors.items():
        out[name] = (out[name] * factor).astype(out[name].dtype)
    return out
```

```python
from contextlib import ExitStack

import numpy as np

import concourse.bass as bass
from concourse import mybir

F32 = mybir.dt.float32
F32R = mybir.dt.float32r
I32 = mybir.dt.int32
U32 = mybir.dt.uint32
ALU = mybir.AluOpType
ACT = mybir.ActivationFunctionType
AX = mybir.AxisListType

P = 128
D = 1024
KC = D // P
SEQ = 64
BATCH = 32
HALVES = 2
TOK = BATCH * SEQ // HALVES
NT = 512
TT = TOK // NT
TB = TOK // P
BPT = NT // P
HD = 128
NKV = 8
GQ = 4
RANK1 = 16
SLOTS = 32
SPT = NT // SEQ
E2, R2 = 8, 16
EF, RF = 16, 64
SM_SCALE = float(HD) ** -0.5
LORA_SCALE = 2.0
FFN_SCALE = 0.5
LANG_BIAS = 5.0
MASKED = -3.0e38

C_ID, C_MASK, C_COS, C_SIN, C_LORA, C_IOTA = 0, 128, 256, 320, 384, 392
C_COLS = 408


def constants():
    t = np.zeros((P, C_COLS), np.float32)
    t[:, C_ID:C_ID + P] = np.eye(P, dtype=np.float32)
    tok = np.arange(P)
    same = tok[:, None] // SEQ == tok[None, :] // SEQ
    t[:, C_MASK:C_MASK + P] = np.where(same & (tok[None, :] <= tok[:, None]), 0.0, MASKED)
    half = HD // 2
    inv_freq = (np.float32(10000.0) ** (-np.arange(half, dtype=np.float32) / np.float32(half))).astype(np.float32)
    ang = np.arange(SEQ, dtype=np.float32)[None, :] * inv_freq[:, None]
    t[:, C_COS:C_COS + SEQ] = np.tile(np.cos(ang), (2, 1))
    t[:half, C_SIN:C_SIN + SEQ] = np.sin(ang)
    t[half:, C_SIN:C_SIN + SEQ] = -np.sin(ang)
    t[:, C_LORA:C_LORA + SPT] = LORA_SCALE * (tok[:, None] // RANK1 == np.arange(SPT)[None, :])
    t[:, C_IOTA:C_IOTA + EF] = np.arange(EF)[None, :]
    return t


RAW_X, RAW_A, RAW_W, RAW_D = 0, 8, 10, 18
PER_G = 10
RAW_3 = RAW_D + PER_G * NKV
RAW_N = RAW_3 + 28
T_X, T_W, T_R2, T_B2, T_A2, T_W2, T_AF, T_F = 0, 8, 16, 17, 18, 19, 27, 28
T_N = 44
S_W, S_D, S_A2, S_W2, S_AF, S_F = 0, 8, 88, 89, 97, 98
S_N = 114
Q_H, Q_C, Q_G = 0, 2, 18
Q_PER_G = 12 + 32
Q_L2 = Q_G + Q_PER_G * NKV
Q_LT2, Q_H2, Q_GT2, Q_Y, Q_AF, Q_LTF, Q_GTF, Q_O = (Q_L2 + i for i in (2, 4, 6, 8, 24, 26, 28, 30))
Q_N = Q_L2 + 62
D_N = PER_G * NKV

H_X, H_W, H_G = 0, 8, 32
H_X1 = H_G + 8 * NKV
H_A2, H_W2, H_F = H_X1 + 16, H_X1 + 17, H_X1 + 42
HI_N = H_F + 24
STEP_N = 27
GATES_N = (16 * E2 + 128, 128)


def raw_count(r):
    n = 16 * (r // 2 + 1)
    if r // 2 >= RAW_A // 2:
        n += 16 * (SPT - 1)
    if r % 2 == 1 and r >= RAW_3 + 1:
        n += 16 * (KC - 1)
    if r % 2 == 1 and r >= RAW_3 + 11:
        n += 16
    return n


RAW_GAIN = [raw_count(RAW_N - 2), raw_count(RAW_N - 1)]


def build(nc, x, ids1, ids2, W1, b1, A1, B1, wq, wk, wv, wo, W2, Wr2, A2, B2, Wf, bf, Af, Bf, Rf, consts, scratch, out):
    with ExitStack() as ctx:
        at = [0]
        BASE = (nc.sbuf_base + 31) // 32 * 32

        def sb(name, shape, dt=F32, offset=None):
            size = 4 * int(np.prod(shape[1:]))
            if offset is None:
                offset = at[0]
                at[0] += (size + 31) // 32 * 32
            return nc.alloc_sbuf_tensor_at(name, shape, dt, offset=BASE + offset)

        KB = 1024
        XH = sb("x_hi", [P, KC * TOK], F32R)
        XL = sb("x_lo", [P, KC * TOK], F32R)
        OH = sb("o_hi", [P, GQ * TOK], F32R, offset=0)
        OL = sb("o_lo", [P, GQ * TOK], F32R, offset=16 * KB)
        K = sb("k_rot", [P, TOK], offset=32 * KB)
        V = sb("v_tok", [P, TB * HD], offset=36 * KB)
        VT = sb("v_feat", [P, NT], offset=40 * KB)
        Q = sb("q_rot", [P, 2 * NT], offset=42 * KB)
        SM = sb("probs", [P, 2 * NT], offset=46 * KB)
        PT = sb("probs_t", [P, 2 * NT], offset=50 * KB)
        RC = sb("rope_cos", [P, 2 * NT], offset=54 * KB)
        RS = sb("rope_sin", [P, 2 * NT], offset=58 * KB)
        NMX = sb("neg_max", [P, 2 * BPT], offset=62 * KB)
        MX = sb("row_max", [P, 2 * BPT], offset=62 * KB + 64)
        SUM = sb("row_sum", [P, 2 * BPT], offset=62 * KB + 128)
        RCP = sb("row_rcp", [P, 2 * BPT], offset=62 * KB + 192)
        CH = sb("c_hi", [P, KC * TOK], F32R)
        CL = sb("c_lo", [P, KC * TOK], F32R)
        X1 = sb("x1", [P, KC * TOK])
        RAW = [sb(f"raw{i}", [P, D]) for i in range(2)]
        WH = [sb(f"w_hi{i}", [P, D], F32R) for i in range(2)]
        WL = [sb(f"w_lo{i}", [P, D], F32R) for i in range(2)]
        buf = at[0]
        at[0] += 12 * KB
        B1S = sb("b1_rows", [P, TT * D], offset=buf)
        HM = sb("h_masked", [P, TT * NT], offset=buf + 8 * KB)
        B2T = sb("b2_t", [P, D], offset=buf)
        H2 = sb("h2", [P, TOK], offset=buf + 4 * KB)
        GT = sb("gates_t", [P, TOK], offset=buf + 8 * KB)
        AF32 = sb("af_out", [P, TOK], offset=buf)
        HF = sb("h_twice", [P, TOK], offset=buf + 4 * KB)
        CB = [GT, sb("comb_b", [P, TOK], offset=buf)]
        OT = [sb(f"out_t{t}", [P, NT], offset=buf + 2 * KB * t) for t in range(TT)]
        OS = [sb(f"out_s{t}", [P, NT], offset=buf + (4 + 2 * t) * KB) for t in range(TT)]
        BC = [sb(f"lora_b{i}", [P, TT * P]) for i in range(2)]
        CT = sb("consts_sb", [P, C_COLS])
        B1C = sb("bias1", [P, KC])
        BFC = sb("biasf", [P, KC])
        ID1 = sb("ids1_sb", [1, BATCH], I32)
        LID = sb("lang_id", [P, HALVES * TB], I32)
        LIDF = sb("lang_idf", [P, HALVES * TB])
        LB = sb("lang_bias", [P, HALVES * TB * E2])
        R2T = sb("router2_t", [P, KC * E2])
        LG = sb("logits", [P, TB * EF])
        PR = sb("route_p", [P, TB * EF])
        GA = sb("gate_a", [P, TB * EF])
        M8 = sb("top8", [P, TB * 8])
        I8 = sb("top8_i", [P, TB * 8], U32)
        I8F = sb("top8_f", [P, TB * 8])
        SC = sb("route_s", [P, 6 * TB])
        assert BASE + at[0] <= nc.SBUF_PARTITION_SIZE_BYTES, at[0]

        PJ = [ctx.enter_context(nc.psum_tensor(f"prod{i}", [P, NT], F32)) for i in range(4)]
        TP = [ctx.enter_context(nc.psum_tensor(f"turned{i}", [P, D], F32)) for i in range(2)]
        SB_ = [TP[0][:, i * NT:(i + 1) * NT] for i in range(2)]
        TBK = TP[1][:, 0:NT]
        OB = TP[1][:, NT:2 * NT]

        def sem(name):
            return ctx.enter_context(nc.semaphore(name))

        const_in = sem("const_in")
        raw_in = [sem("raw_in0"), sem("raw_in1")]
        b1_in = sem("b1_in")
        gates_out = sem("gates_out")
        gates_in = [sem("gates_in0"), sem("gates_in1")]
        out_done = [sem("out_done0"), sem("out_done1")]
        turned = sem("turned")
        split_t = sem("split_t")
        split_d = sem("split_d")
        wd_hi = sem("wd_hi")
        wf_used = sem("wf_used")
        hi_done = sem("hi_done")
        prod = sem("prod")
        taken = sem("taken")
        bc_in = sem("bc_in")
        x_res = sem("x_res")
        qk_in = sem("qk_in")
        scores = sem("scores")
        s_masked = sem("s_masked")
        max_in = sem("max_in")
        nmax_in = sem("nmax_in")
        exp_in = sem("exp_in")
        rcp_in = sem("rcp_in")
        probs_in = sem("probs_in")
        tb_done = sem("tb_done")
        tb_taken = sem("tb_taken")
        pv_done = sem("pv_done")
        o_split = sem("o_split")
        x1_lo = sem("x1_lo")
        step = sem("dve_step")
        logits_in = sem("logits_in")
        rexp = sem("route_exp")
        gates_in_sb = sem("gates_tok")
        hm2_in = sem("hm2_in")
        hf_in = sem("hf_in")
        g_prod = sem("g_prod")
        g_split = sem("g_split")

        held = {e.engine: sem(f"held_{n}") for n, e in (("sp", nc.sync), ("pe", nc.tensor), ("act", nc.scalar),
                                                        ("pool", nc.gpsimd), ("dve", nc.vector))}

        ident = CT[:, C_ID:C_ID + P]
        iota = CT[:, C_IOTA:C_IOTA + EF]

        block = ctx.enter_context(nc.Block())

        def view(t, n, lo=0, hi=None):
            v = t.rearrange("p (n m) -> p n m", n=n)
            return v[:, :, lo:hi] if hi is not None else v

        def hold(eng):
            eng.sem_inc(held[eng.engine], 1)

        def per_half(eng, hf):
            return (eng.snap(hf * Q_N), eng.snap(hf * T_N))

        @block.sync
        def _(sp):
            for t in range(TT):
                sp.sem_inc(out_done[t], 16)
            sp.dma_start(CT[:], consts).then_inc(const_in, 16)
            sp.dma_start(B1C[:], b1).then_inc(const_in, 16)
            sp.dma_start(BFC[:], bf).then_inc(const_in, 16)
            sp.dma_start(ID1[:], ids1.rearrange("(a b) -> a b", a=1)).then_inc(const_in, 16)
            for s in range(2):
                sp.dma_start(LID[s * SEQ:(s + 1) * SEQ, :],
                             ids2[s:s + 1, :].to_broadcast([SEQ, HALVES * TB])).then_inc(const_in, 16)

            with sp.Fori(0, HALVES) as hf:
                q_base, t_base = per_half(sp, hf)
                d_base = sp.snap(hf * D_N)

                def load(s, src, dst=None):
                    sp.dma_start(RAW[s][:] if dst is None else dst, src).then_inc(raw_in[s], 16)

                def free_of_t(k):
                    sp.wait_ge(turned, t_base + (k - 1 + 2))
                    hold(sp)

                with sp.Fori(0, TB // 2) as i:
                    for s in range(2):
                        sp.wait_ge(turned, t_base + i * 2 + (T_X + s - 1 + 2))
                        load(s, x[bass.ds(hf * TOK + i * (2 * P) + s * P, P), :])
                sp.wait_ge(const_in, 16 * 6)
                for t in range(TT):
                    sp.wait_ge(out_done[t], hf * (16 * KC) + 16)
                for t in range(TT):
                    sp.wait_ge(turned, t_base + (T_X + 6 + t + 1 + 2))
                    raw3 = RAW[t][:].rearrange("p (k m) -> p k m", k=KC)
                    for n in range(SPT):
                        m = sp.value_load(ID1[0:1, bass.ds(hf * (BATCH // HALVES) + (t * SPT + n), 1)],
                                          min_val=0, max_val=SLOTS - 1)
                        sp.dma_start(raw3[:, :, n * RANK1:(n + 1) * RANK1],
                                     A1[bass.ds(m * D, D), :].rearrange("(k p) r -> p k r", p=P)
                                     ).then_inc(raw_in[t], 16)
                        sp.dma_start(B1S[n * RANK1:(n + 1) * RANK1, t * D:(t + 1) * D],
                                     B1[bass.ds(m * RANK1, RANK1), :]).then_inc(b1_in, 16)
                for j in range(2):
                    sp.wait_ge(prod, q_base + (Q_H + j + 1))
                    load(j, W1[j * P:(j + 1) * P, :])
                with sp.Fori(1, KC // 2) as i:
                    for s in range(2):
                        sp.wait_ge(turned, t_base + i * 2 + (T_W + s - 1 + 2))
                        load(s, W1[bass.ds(i * (2 * P) + s * P, P), :])
                free_of_t(T_W + KC + 1)
                with sp.Fori(0, NKV) as g:
                    dg = sp.snap(d_base + g * PER_G)

                    def col(w, c):
                        return w.rearrange("(k p) n -> p k n", p=P)[:, :, bass.ds(c, P)]

                    srcs = [col(wk, g * P), col(wv, g * P)]
                    srcs += [col(wq, g * (GQ * P) + h * P) for h in range(GQ)]
                    for hh in range(2):
                        for oc in range(2):
                            srcs.append(wo[bass.ds(g * (GQ * HD) + hh * 2 * HD, 2 * HD),
                                           oc * NT:(oc + 1) * NT].rearrange("(h d) n -> d h n", d=HD))
                    for j, src in enumerate(srcs):
                        sp.wait_ge(split_d, dg + (j - 1 + 2))
                        load(j % 2, src, view(RAW[j % 2][:], 2 if j >= 6 else KC))
                sp.wait_ge(split_d, d_base + (D_N + 2))
                load(0, Wr2, RAW[0][0:E2, :])
                raw_b2 = RAW[1][:].rearrange("p (c e r) -> p c e r", c=KC, e=E2)
                for c in range(KC):
                    load(1, B2[:, c * P:(c + 1) * P, :].rearrange("e p r -> p e r"), raw_b2[:, c])
                free_of_t(T_A2)
                load(0, A2)
                with sp.Fori(0, KC // 2) as i:
                    for s in range(2):
                        sp.wait_ge(turned, t_base + i * 2 + (T_W2 + s - 1 + 2))
                        load(1 - s, W2[bass.ds(i * (2 * P) + s * P, P), :])
                free_of_t(T_AF)
                load(1, Af, RAW[1][0:RF, :])
                load(1, Rf, RAW[1][RF:RF + EF, :])
                with sp.Fori(0, KC) as o:
                    sp.wait_ge(turned, t_base + o * 2 + (T_F - 1 + 2))
                    load(0, Wf[bass.ds(o * P, P), :])
                    sp.wait_ge(turned, t_base + o * 2 + (T_F + 2))
                    load(1, Bf[:, bass.ds(o * P, P), :].rearrange("e p r -> p e r"),
                         RAW[1][:].rearrange("p (e r) -> p e r", e=EF))
            for t in range(TT):
                sp.wait_ge(out_done[t], HALVES * KC * 16 + 16)

        @block.tensor
        def _(pe):
            pe.sem_inc(turned, 2)
            pe.wait_ge(const_in, 16 * 6)
            hold(pe)
            with pe.Fori(0, HALVES) as hf:
                q_base, t_base = per_half(pe, hf)
                r_base = [pe.snap(hf * RAW_GAIN[s]) for s in range(2)]

                def raw_ready(s, off):
                    pe.wait_ge(raw_in[s], r_base[s] + off)

                def turn(par, k, rows=P, width=P, ready=None, base=None):
                    ready()
                    pe.wait_ge(split_t, (t_base if base is None else base) + (k - 1 + 2))
                    if rows < P:
                        hold(pe)
                    for c in range(KC):
                        mm = pe.transpose(TP[par][:, c * width:c * width + rows],
                                          RAW[par][0:rows, c * P:(c + 1) * P], ident[0:rows, 0:rows])
                    mm.then_inc(turned, 1)

                def three(dst, wh, wl, xh, xl, start, stop):
                    pe.matmul(dst, wh, xh, start=start, stop=False)
                    pe.matmul(dst, wh, xl, start=False, stop=False)
                    return pe.matmul(dst, wl, xh, start=False, stop=stop)

                def main(q, s, t, XHi, XLo, start=True, stop=True, m=P):
                    for k in range(KC):
                        xs = slice(k * TOK + t * NT, k * TOK + (t + 1) * NT)
                        ws = slice(k * P, k * P + m)
                        mm = three(PJ[q % 4][0:m, :], WH[s][:, ws], WL[s][:, ws], XHi[:, xs], XLo[:, xs],
                                   start and k == 0, stop and k == KC - 1)
                    return mm

                def bank_free(q, base=None):
                    pe.wait_ge(taken, (q_base if base is None else base) + (q + 1))
                    hold(pe)

                with pe.Fori(0, TB // 2) as i:
                    tb = pe.snap(t_base + i * 2)
                    rb = [pe.snap(r_base[s] + i * 16) for s in range(2)]
                    for s in range(2):
                        turn(s, T_X + s, ready=lambda: pe.wait_ge(raw_in[s], rb[s] + 16), base=tb)
                for t in range(TT):
                    raw_ready(t, raw_count(RAW_A + t))
                    pe.wait_ge(x_res, hf * TB + (t + 1) * (TB // TT))
                    bank_free(Q_H + t)
                    for k in range(KC):
                        mm = pe.matmul(PJ[(Q_H + t) % 4][:], RAW[t][:, k * P:(k + 1) * P],
                                       X1[:, k * TOK + t * NT:k * TOK + (t + 1) * NT],
                                       start=(k == 0), stop=(k == KC - 1))
                    mm.then_inc(prod, 1)

                def with_lora(s, qb, b_col, h, first, h_ready=lambda: None):
                    for t in range(TT):
                        bank_free(first + t, qb)
                        main(first + t, s, t, XH, XL, stop=False)
                    h_ready()
                    for t in range(TT):
                        pe.matmul(PJ[(first + t) % 4][:], BC[s][:, b_col(t):b_col(t) + P], h(t),
                                  start=False, stop=True).then_inc(prod, 1)

                turn(0, T_W, ready=lambda: raw_ready(0, raw_count(RAW_W)))
                pe.wait_ge(taken, q_base + (Q_H + TT + 4))
                hold(pe)

                def w1_block(s, tb, rb, qb, bcb, last=False):
                    if not last:
                        turn(1 - s, T_W + s + 1, base=tb,
                             ready=lambda: pe.wait_ge(raw_in[1 - s], rb[1 - s] + raw_count(RAW_W + 1 + s)))
                    pe.wait_ge(split_t, tb + (T_W + s + 1 + 2))
                    pe.wait_ge(bc_in, bcb + (s + 1))
                    with_lora(s, qb, lambda t: t * P, lambda t: HM[:, t * NT:(t + 1) * NT], Q_C + 2 * s)

                with pe.Fori(0, KC // 2 - 1) as i:
                    bases = (pe.snap(t_base + i * 2), [pe.snap(r_base[s] + i * 16) for s in range(2)],
                             pe.snap(q_base + i * 4), pe.snap(hf * (2 * KC) + i * 2))
                    for s in range(2):
                        w1_block(s, *bases)
                i = KC // 2 - 1
                bases = (pe.snap(t_base + i * 2), [pe.snap(r_base[s] + i * 16) for s in range(2)],
                         pe.snap(q_base + i * 4), pe.snap(hf * (2 * KC) + i * 2))
                for s in range(2):
                    w1_block(s, *bases, last=(s == 1))

                pe.wait_ge(taken, q_base + (Q_G + 4))
                hold(pe)
                with pe.Fori(0, NKV) as g:
                    qg = pe.snap(q_base + g * Q_PER_G)
                    dg = pe.snap(hf * D_N + g * PER_G)
                    ug = pe.snap(hf * (NKV * 8) + g * 8)
                    kg = pe.snap(hf * (NKV * 10) + g * 10)

                    def turn_v(t):
                        pe.wait_ge(taken, qg + (Q_G + TT + t + 1 + 4))
                        pe.wait_ge(tb_taken, kg + (t + 1))
                        for b in range(BPT):
                            mm = pe.transpose(TBK[:, b * P:(b + 1) * P], VT[:, b * P:(b + 1) * P], ident)
                        mm.then_inc(tb_done, 1)

                    def score(u):
                        pe.wait_ge(qk_in, kg + (TT + u + 1))
                        pe.wait_ge(s_masked, ug + (u + 1))
                        t = u % TT
                        for b in range(BPT):
                            mm = pe.matmul(SB_[u % 2][:, b * P:(b + 1) * P],
                                           Q[:, (u % 2) * NT + b * P:(u % 2) * NT + (b + 1) * P],
                                           K[:, t * NT + b * P:t * NT + (b + 1) * P], start=True, stop=True)
                        mm.then_inc(scores, 1)

                    def turn_p(u):
                        pe.wait_ge(probs_in, ug + (u + 1))
                        pe.wait_ge(tb_taken, kg + (TT + u + 1))
                        for b in range(BPT):
                            c = (u % 2) * NT + b * P
                            mm = pe.transpose(TBK[:, b * P:(b + 1) * P], SM[:, c:c + P], ident)
                        mm.then_inc(tb_done, 1)

                    def pv(u):
                        pe.wait_ge(tb_taken, kg + (TT + u + 1 + 1))
                        pe.wait_ge(o_split, ug + (u + 1))
                        t = u % TT
                        for b in range(BPT):
                            c = (u % 2) * NT + b * P
                            mm = pe.matmul(OB[:, b * P:(b + 1) * P], V[:, (t * BPT + b) * HD:(t * BPT + b + 1) * HD],
                                           PT[:, c:c + P], start=True, stop=True)
                        mm.then_inc(pv_done, 1)

                    def attention(j):
                        if 0 <= j - 5 < 8:
                            score(j - 5)
                        if 0 <= j - 6 < 8:
                            turn_p(j - 6)
                        if 0 <= j - 7 < 8:
                            pv(j - 7)

                    for j in range(12):
                        if j % TT == 0:
                            pe.wait_ge(split_d, dg + (j // TT + 1 + 2))
                        bank_free(Q_G + j, qg)
                        main(Q_G + j, (j // TT) % 2, j % TT, CH, CL).then_inc(prod, 1)
                        if j in (3, 4):
                            turn_v(j - 3)
                        attention(j)
                    for i in range(32):
                        hh, oc, o4, t = i // 16, i // 8 % 2, i // 2 % 4, i % 2
                        if i % 8 == 0:
                            pe.wait_ge(split_d, dg + (6 + i // 8 + 1 + 2))
                        if i % 16 == 0:
                            pe.wait_ge(o_split, ug + (4 * (hh + 1) + 1))
                        q = Q_G + 12 + i
                        bank_free(q, qg)
                        s = (i // 8) % 2
                        for h2 in range(2):
                            ws = slice(h2 * NT + o4 * P, h2 * NT + (o4 + 1) * P)
                            xs = slice((2 * hh + h2) * TOK + t * NT, (2 * hh + h2) * TOK + (t + 1) * NT)
                            mm = three(PJ[q % 4][:], WH[s][:, ws], WL[s][:, ws], OH[:, xs], OL[:, xs],
                                       h2 == 0, h2 == 1)
                        mm.then_inc(prod, 1)
                        if i in (3, 7, 11):
                            attention(12 + i // 4)

                turn(0, T_R2, rows=E2, width=E2, ready=lambda: raw_ready(0, raw_count(RAW_3)))
                turn(1, T_B2, ready=lambda: raw_ready(1, raw_count(RAW_3 + 1)))
                pe.wait_ge(taken, q_base + (Q_L2 + 4))
                pe.wait_ge(split_t, t_base + (T_R2 + 1 + 2))
                for t in range(TT):
                    for k in range(KC):
                        mm = pe.matmul(PJ[(Q_L2 + t) % 4][0:E2, :], R2T[:, k * E2:(k + 1) * E2],
                                       X1[:, k * TOK + t * NT:k * TOK + (t + 1) * NT],
                                       start=(k == 0), stop=(k == KC - 1))
                    mm.then_inc(prod, 1)
                turn(0, T_A2, ready=lambda: raw_ready(0, raw_count(RAW_3 + 2)))
                for t in range(TT):
                    pe.wait_ge(taken, q_base + (Q_L2 + t + 1 + 4))
                    hold(pe)
                    for b in range(BPT):
                        mm = pe.transpose(PJ[(Q_LT2 + t) % 4][:, b * E2:(b + 1) * E2],
                                          GT[0:E2, t * NT + b * P:t * NT + (b + 1) * P], ident[0:E2, 0:E2])
                    mm.then_inc(prod, 1)
                pe.wait_ge(split_t, t_base + (T_A2 + 1 + 2))
                for t in range(TT):
                    pe.wait_ge(x1_lo, hf * (TT * KC) + (t + 1) * KC)
                    bank_free(Q_H2 + t)
                    main(Q_H2 + t, 0, t, XH, XL).then_inc(prod, 1)

                def turn_gates(q, e):
                    for t in range(TT):
                        bank_free(q + t)
                        for b in range(BPT):
                            c = (t * BPT + b) * e
                            mm = pe.transpose(PJ[(q + t) % 4][0:e, b * P:(b + 1) * P], GA[:, c:c + e], ident)
                        mm.then_inc(prod, 1)

                pe.wait_ge(gates_in_sb, hf * 2 + 1)
                turn_gates(Q_GT2, E2)
                turn(1, T_W2, ready=lambda: raw_ready(1, raw_count(RAW_3 + 3)))

                def w2_block(s, tb, rb, qb, bcb, last=False):
                    turn(s, T_W2 + s + 1, base=tb, rows=RF + EF if last else P,
                         ready=lambda: pe.wait_ge(raw_in[s], rb[s] + raw_count(RAW_3 + 4 + s) + (16 if last else 0)))
                    pe.wait_ge(split_t, tb + (T_W2 + s + 1 + 2))
                    pe.wait_ge(bc_in, bcb + (KC + s + 1))
                    with_lora(1 - s, qb, lambda t: 0, lambda t: H2[:, t * NT:(t + 1) * NT], Q_Y + 2 * s,
                              lambda: pe.wait_ge(hm2_in, hf + 1))

                with pe.Fori(0, KC // 2 - 1) as i:
                    bases = (pe.snap(t_base + i * 2), [pe.snap(r_base[s] + i * 16) for s in range(2)],
                             pe.snap(q_base + i * 4), pe.snap(hf * (2 * KC) + i * 2))
                    for s in range(2):
                        w2_block(s, *bases)
                i = KC // 2 - 1
                bases = (pe.snap(t_base + i * 2), [pe.snap(r_base[s] + i * 16) for s in range(2)],
                         pe.snap(q_base + i * 4), pe.snap(hf * (2 * KC) + i * 2))
                for s in range(2):
                    w2_block(s, *bases, last=(s == 1))

                turn(0, T_F, ready=lambda: raw_ready(0, raw_count(RAW_3 + 12)))
                pe.wait_ge(split_t, t_base + (T_AF + 1 + 2))
                m = RF + EF
                for t in range(TT):
                    pe.wait_ge(taken, q_base + (Q_Y + 2 * KC - 1 + t + 4))
                    main(Q_AF + t, 1, t, CH, CL, m=m).then_inc(prod, 1)
                for t in range(TT):
                    pe.wait_ge(taken, q_base + (Q_AF + t + 1 + 4))
                    for b in range(BPT):
                        mm = pe.transpose(PJ[(Q_LTF + t) % 4][:, b * m:(b + 1) * m],
                                          AF32[0:m, t * NT + b * P:t * NT + (b + 1) * P], ident[0:m, 0:m])
                    mm.then_inc(prod, 1)
                pe.wait_ge(gates_in_sb, hf * 2 + 2)
                turn_gates(Q_GTF, EF)

                def turn_out(q, qb):
                    for t in range(TT):
                        pe.wait_ge(taken, qb + (q - 2 + t + 1 + 4))
                        for b in range(BPT):
                            mm = pe.transpose(PJ[(q + t) % 4][:, b * P:(b + 1) * P],
                                              OT[t][:, b * P:(b + 1) * P], ident)
                        mm.then_inc(prod, 1)

                def ffn_block(tb, rb, qb, first=False, last=False):
                    turn(1, T_F + 1, base=tb, ready=lambda: pe.wait_ge(raw_in[1], rb[1] + raw_count(RAW_3 + 13)))
                    pe.wait_ge(split_t, tb + (T_F + 1 + 2))
                    for t in range(TT):
                        bank_free(Q_O + t, qb)
                        mm = main(Q_O + t, 0, t, CH, CL, stop=False)
                    mm.then_inc(wf_used, 1)
                    if not last:
                        turn(0, T_F + 2, base=tb, ready=lambda: pe.wait_ge(raw_in[0], rb[0] + raw_count(RAW_3 + 14)))
                    if not first:
                        turn_out(Q_O - 2, qb)
                    pe.wait_ge(split_t, tb + (T_F + 2 + 2))
                    for t in range(TT):
                        for k in range(KC):
                            if first and t == 0:
                                pe.wait_ge(g_split, hf * KC + (k + 1 + 2))
                            xs = slice(k * TOK + t * NT, k * TOK + (t + 1) * NT)
                            ws = slice(k * P, (k + 1) * P)
                            mm = three(PJ[(Q_O + t) % 4][:], WH[1][:, ws], WL[1][:, ws], XH[:, xs], XL[:, xs],
                                       False, k == KC - 1)
                        mm.then_inc(prod, 1)

                ffn_block(t_base, r_base, q_base, first=True)
                with pe.Fori(1, KC - 1) as o:
                    ffn_block(pe.snap(t_base + o * 2), [pe.snap(r_base[s] + o * 16) for s in range(2)],
                              pe.snap(q_base + o * 4))
                o = KC - 1
                ffn_block(pe.snap(t_base + o * 2), [pe.snap(r_base[s] + o * 16) for s in range(2)],
                          pe.snap(q_base + o * 4), last=True)
                turn_out(Q_O + 4 * KC - 2, q_base)

        @block.scalar
        def _(act):
            act.sem_inc(tb_taken, 1)
            act.wait_ge(const_in, 16 * 6)
            hold(act)
            with act.Fori(0, HALVES) as hf:
                q_base, t_base = per_half(act, hf)
                d_base = act.snap(hf * D_N)

                def is_turned(k, base=None):
                    act.wait_ge(turned, (t_base if base is None else base) + (k + 1 + 2))

                def is_prod(q, base=None):
                    act.wait_ge(prod, (q_base if base is None else base) + (q + 1))

                def w_hi(par, cols=P):
                    act.copy(view(WH[par][:], KC, 0, cols), view(TP[par][:], KC, 0, cols)).then_inc(hi_done, 1)

                with act.Fori(0, TB // 2) as i:
                    tb = act.snap(t_base + i * 2)
                    for s in range(2):
                        is_turned(T_X + s, tb)
                        act.copy(view(XH[:], KC)[:, :, bass.ds(i * (2 * P) + s * P, P)], view(TP[s][:], KC)
                                 ).then_inc(hi_done, 1)
                is_turned(T_W)
                w_hi(0)
                act.wait_ge(b1_in, hf * (16 * TT * SPT) + 16 * TT * SPT)

                def b1_cols(s, j):
                    act.copy(view(BC[s][:], TT), view(B1S[:], TT)[:, :, bass.ds(j, P)]).then_inc(bc_in, 1)

                b1_cols(0, 0)

                def w1_block(s, i, tb, qb, last=False):
                    if not last:
                        is_turned(T_W + s + 1, tb)
                        act.wait_ge(prod, qb + (Q_C + 2 * s))
                        w_hi(1 - s)
                        b1_cols(1 - s, i * (2 * P) + (s + 1) * P)
                    for t in range(TT):
                        is_prod(Q_C + 2 * s + t, qb)
                        act.activation(CH[:, bass.ds(i * (2 * TOK) + s * TOK + t * NT, NT)], PJ[(Q_C + 2 * s + t) % 4][:],
                                       ACT.Identity, bias=B1C[:, bass.ds(i * 2 + s, 1)]).then_inc(hi_done, 1)

                with act.Fori(0, KC // 2 - 1) as i:
                    bases = act.snap(t_base + i * 2), act.snap(q_base + i * 4)
                    for s in range(2):
                        w1_block(s, i, *bases)
                i = KC // 2 - 1
                bases = act.snap(t_base + i * 2), act.snap(q_base + i * 4)
                for s in range(2):
                    w1_block(s, i, *bases, last=(s == 1))

                with act.Fori(0, NKV) as g:
                    ug = act.snap(hf * (NKV * 8) + g * 8)
                    kg = act.snap(hf * (NKV * 10) + g * 10)

                    def take_v(t):
                        act.wait_ge(tb_done, kg + (t + 1))
                        act.copy(V[:, t * BPT * HD:(t + 1) * BPT * HD], TBK).then_inc(tb_taken, 1)

                    def attention(j):
                        if 0 <= j - 6 < 8:
                            u = j - 6
                            act.wait_ge(tb_done, kg + (TT + u + 1))
                            if u >= 2:
                                act.wait_ge(pv_done, ug + (u - 1))
                            act.copy(PT[:, (u % 2) * NT:(u % 2 + 1) * NT], TBK).then_inc(tb_taken, 1)
                        if 0 <= j - 7 < 8:
                            u = j - 7
                            act.wait_ge(pv_done, ug + (u + 1))
                            c = (u // 2) * TOK + (u % 2) * NT
                            act.copy(OH[:, c:c + NT], OB).then_inc(hi_done, 1)
                        if 0 <= j - 5 < 8:
                            u = j - 5
                            act.wait_ge(nmax_in, ug + (u + 1))
                            for b in range(BPT):
                                c, r = (u % 2) * NT + b * P, (u % 2) * BPT + b
                                ins = act.activation(SM[:, c:c + P], SM[:, c:c + P], ACT.Exp, bias=NMX[:, r:r + 1],
                                                     scale=SM_SCALE, accum_out=SUM[:, r:r + 1])
                            ins.then_inc(exp_in, 1)

                    take_v(0)
                    take_v(1)
                    for j in range(5, 15):
                        attention(j)

                act.wait_ge(taken, q_base + (Q_L2 + 4))
                for t in range(TT):
                    for k in range(KC):
                        xs = slice(k * TOK + t * NT, k * TOK + (t + 1) * NT)
                        act.copy(XH[:, xs], X1[:, xs]).then_inc(hi_done, 1)
                is_turned(T_A2)
                w_hi(0)
                act.wait_ge(logits_in, hf * 2 + 1)
                act.activation(SC[:, TB:2 * TB], SC[:, 0:TB], ACT.Exp).then_inc(rexp, 1)
                is_turned(T_W2)
                w_hi(1)

                def b2_cols(s, c):
                    act.copy(BC[s][:, 0:P], B2T[:, bass.ds(c, P)]).then_inc(bc_in, 1)

                act.wait_ge(split_t, t_base + (T_B2 + 1 + 2))
                b2_cols(1, 0)

                def w2_block(s, i, tb, qb, last=False):
                    is_turned(T_W2 + s + 1, tb)
                    act.wait_ge(prod, qb + (Q_Y + 2 * s))
                    w_hi(s, RF + EF if last else P)
                    if not last:
                        b2_cols(s, i * (2 * P) + (s + 1) * P)
                    for t in range(TT):
                        is_prod(Q_Y + 2 * s + t, qb)
                        act.copy(CH[:, bass.ds(i * (2 * TOK) + s * TOK + t * NT, NT)], PJ[(Q_Y + 2 * s + t) % 4][:]
                                 ).then_inc(hi_done, 1)

                with act.Fori(0, KC // 2 - 1) as i:
                    bases = act.snap(t_base + i * 2), act.snap(q_base + i * 4)
                    for s in range(2):
                        w2_block(s, i, *bases)
                i = KC // 2 - 1
                bases = act.snap(t_base + i * 2), act.snap(q_base + i * 4)
                for s in range(2):
                    w2_block(s, i, *bases, last=(s == 1))

                is_turned(T_F)
                w_hi(0)
                for t in range(TT):
                    is_prod(Q_AF + t)
                    for half in range(2):
                        ins = act.copy(HF[half * RF:(half + 1) * RF, t * NT:(t + 1) * NT],
                                       PJ[(Q_AF + t) % 4][0:RF, :])
                    ins.then_inc(hf_in, 1)
                act.wait_ge(logits_in, hf * 2 + 2)
                act.activation(PR[:], PR[:], ACT.Exp).then_inc(rexp, 1)
                is_turned(T_F + 1)
                w_hi(1)
                for c in range(KC):
                    act.wait_ge(g_prod, hf * KC + (c + 1))
                    act.copy(XH[:, c * TOK:(c + 1) * TOK], CB[c % 2][:]).then_inc(hi_done, 1)
                is_turned(T_F + 2)
                act.wait_ge(wf_used, hf * KC + 1)
                w_hi(0)

                def store(o, q, qb):
                    for t in range(TT):
                        act.wait_ge(taken, qb + (q + t + 1 + 4))
                        act.dma_start(out[bass.ds(hf * TOK + t * NT, NT), bass.ds(o * P, P)]
                                      .rearrange("(b p) n -> p b n", p=P),
                                      view(OS[t][:], BPT)).then_inc(out_done[t], 16)

                def ffn_block(o, tb, qb, last=False):
                    is_turned(T_F + 1, tb)
                    act.wait_ge(prod, qb + (Q_O - 2))
                    w_hi(1)
                    if not last:
                        is_turned(T_F + 2, tb)
                        act.wait_ge(wf_used, hf * KC + o + 1)
                        w_hi(0)
                    store(o - 1, Q_O - 2, qb)

                with act.Fori(1, KC - 1) as o:
                    ffn_block(o, act.snap(t_base + o * 2), act.snap(q_base + o * 4))
                o = KC - 1
                ffn_block(o, act.snap(t_base + o * 2), act.snap(q_base + o * 4), last=True)
                store(KC - 1, Q_O + 4 * KC - 2, q_base)

        @block.gpsimd
        def _(pool):
            pool.sem_inc(split_d, 2)
            with pool.Fori(0, HALVES) as hf:
                q_base, t_base = per_half(pool, hf)
                with pool.Fori(0, TB) as i:
                    pool.wait_ge(split_t, t_base + i + (T_X + 1 + 2))
                    hold(pool)
                    xs = bass.ds(i * P, P)
                    pool.tensor_tensor(view(X1[:], KC)[:, :, xs], view(XH[:].bitcast(F32), KC)[:, :, xs],
                                       view(XL[:].bitcast(F32), KC)[:, :, xs], ALU.add).then_inc(x_res, 1)
                pool.wait_ge(prod, q_base + (Q_C + 14))
                hold(pool)
                last_use = (-8, 0, 2, 4, 6, 8, 10, 12, 20, 28)
                with pool.Fori(0, NKV) as g:
                    qg = pool.snap(q_base + g * Q_PER_G)
                    dg = pool.snap(hf * D_N + g * PER_G)
                    rg = [pool.snap(hf * RAW_GAIN[s] + g * (8 * PER_G)) for s in range(2)]
                    for j in range(PER_G):
                        s = j % 2
                        pool.wait_ge(raw_in[s], rg[s] + raw_count(RAW_D + j))
                        pool.wait_ge(prod, qg + (Q_G + last_use[j]))
                        hold(pool)
                        pool.tensor_copy(WH[s][:], RAW[s][:]).then_inc(wd_hi, 1)
                        pool.wait_ge(wd_hi, dg + (j + 1))
                        hold(pool)
                        pool.tensor_tensor(WL[s][:], RAW[s][:], WH[s][:].bitcast(F32), ALU.subtract
                                           ).then_inc(split_d, 1)

                def spread(buf_, row, rank, s):
                    for e in range(P // rank):
                        pool.dma_start(buf_[e * rank:(e + 1) * rank, :],
                                       scratch[bass.ds(row + e, 1), :].to_broadcast([rank, TOK])
                                       ).then_inc(gates_in[s], 16)

                pool.wait_ge(taken, q_base + (Q_GT2 + TT + 4))
                hold(pool)
                pool.dma_start(scratch[0:E2, :], GT[0:E2, :]).then_inc(gates_out, 16)
                pool.wait_ge(gates_out, hf * 32 + 16)
                hold(pool)
                spread(GT, 0, R2, 0)
                pool.wait_ge(taken, q_base + (Q_GTF + TT + 4))
                hold(pool)
                pool.dma_start(scratch[E2:E2 + EF, :], GT[0:EF, :]).then_inc(gates_out, 16)
                pool.wait_ge(gates_out, hf * 32 + 32)
                pool.wait_ge(hf_in, hf * TT + TT)
                hold(pool)
                with pool.Fori(0, KC // 2) as i:
                    for s in range(2):
                        pool.wait_ge(g_split, hf * KC + i * 2 + (s - 1 + 2))
                        hold(pool)
                        spread(CB[s], E2 + i * 4 + 2 * s, RF, s)
                    for s in range(2):
                        pool.wait_ge(gates_in[s], hf * GATES_N[s] + i * 32 + (32 + GATES_N[s] - 128))
                        hold(pool)
                        pool.tensor_tensor(CB[s][:], CB[s][:], HF[:], ALU.mult).then_inc(g_prod, 1)

        @block.vector
        def _(dve):
            dve.sem_inc(taken, 4)
            dve.sem_inc(split_t, 2)
            dve.sem_inc(s_masked, 2)
            dve.sem_inc(o_split, 1)
            dve.sem_inc(g_split, 2)
            dve.wait_ge(const_in, 16 * 6)
            steps = [0]

            def chain(base, ins):
                ins.then_inc(step, 1)
                steps[0] += 1
                dve.wait_ge(step, base + steps[0])

            n = HALVES * TB
            chain(0, dve.tensor_copy(LIDF[:], LID[:]))
            lb3 = view(LB[:], n)
            chain(0, dve.tensor_tensor(lb3, iota[:, 0:E2].unsqueeze(1).to_broadcast([P, n, E2]),
                                       LIDF[:].unsqueeze(2).to_broadcast([P, n, E2]), ALU.is_equal))
            chain(0, dve.tensor_scalar(LB[:], LB[:], LANG_BIAS, None, ALU.mult))

            with dve.Fori(0, HALVES) as hf:
                q_base, t_base = per_half(dve, hf)
                h_base = dve.snap(hf * HI_N)
                s_base = dve.snap(hf * STEP_N + 3)
                steps[0] = 0

                def hi_is(n, base=None):
                    dve.wait_ge(hi_done, (h_base if base is None else base) + (n + 1))

                def is_prod(q, base=None):
                    dve.wait_ge(prod, (q_base if base is None else base) + (q + 1))

                def w_lo(par, cols=P):
                    dve.tensor_tensor(view(WL[par][:], KC, 0, cols), view(TP[par][:], KC, 0, cols),
                                      view(WH[par][:].bitcast(F32), KC, 0, cols), ALU.subtract).then_inc(split_t, 1)

                with dve.Fori(0, TB // 2) as i:
                    hb = dve.snap(h_base + i * 2)
                    for s in range(2):
                        hi_is(H_X + s, hb)
                        xs = bass.ds(i * (2 * P) + s * P, P)
                        dve.tensor_tensor(view(XL[:], KC)[:, :, xs], view(TP[s][:], KC),
                                          view(XH[:].bitcast(F32), KC)[:, :, xs], ALU.subtract).then_inc(split_t, 1)
                for t in range(TT):
                    is_prod(Q_H + t)
                    dve.tensor_tensor(view(HM[:, t * NT:(t + 1) * NT], SPT), view(PJ[(Q_H + t) % 4][:], SPT),
                                      CT[:, C_LORA:C_LORA + SPT].unsqueeze(2).to_broadcast([P, SPT, SEQ]),
                                      ALU.mult).then_inc(taken, 1)
                hi_is(H_W)
                w_lo(0)

                def c_lo(i, s, t, n, q, qb, hb, bias):
                    hi_is(n, hb)
                    cs = bass.ds(i * (2 * TOK) + s * TOK + t * NT, NT)
                    src, hi = PJ[q % 4][:], CH[:].bitcast(F32)[:, cs]
                    if bias is None:
                        ins = dve.tensor_tensor(CL[:, cs], src, hi, ALU.subtract)
                    else:
                        ins = dve.scalar_tensor_tensor(out=CL[:, cs], in0=src, scalar=bias, in1=hi,
                                                       op0=ALU.add, op1=ALU.subtract)
                    ins.then_inc(taken, 1)

                def w1_block(s, i, hb, qb, last=False):
                    n = H_W + 1 + 3 * s
                    if not last:
                        hi_is(n, hb)
                        w_lo(1 - s)
                        n += 1
                    for t in range(TT):
                        c_lo(i, s, t, n + t, Q_C + 2 * s + t, qb, hb, B1C[:, bass.ds(i * 2 + s, 1)])

                with dve.Fori(0, KC // 2 - 1) as i:
                    bases = dve.snap(h_base + i * 6), dve.snap(q_base + i * 4)
                    for s in range(2):
                        w1_block(s, i, *bases)
                i = KC // 2 - 1
                bases = dve.snap(h_base + i * 6), dve.snap(q_base + i * 4)
                for s in range(2):
                    w1_block(s, i, *bases, last=(s == 1))

                dve.wait_ge(x_res, hf * TB + TB)
                hold(dve)
                with dve.Fori(0, NKV) as g:
                    qg = dve.snap(q_base + g * Q_PER_G)
                    hg = dve.snap(h_base + g * 8)
                    ug = dve.snap(hf * (NKV * 8) + g * 8)
                    kg = dve.snap(hf * (NKV * 10) + g * 10)
                    cos = CT[:, C_COS:C_COS + SEQ].unsqueeze(1).to_broadcast([P, SPT, SEQ])
                    hd2 = HD // 2

                    def rotate(j, dst):
                        is_prod(Q_G + j, qg)
                        src = view(PJ[(Q_G + j) % 4][:], SPT)
                        rs = slice((j % 2) * NT, (j % 2 + 1) * NT)
                        dve.tensor_tensor(view(RC[:, rs], SPT), src, cos, ALU.mult)
                        for a, b in ((0, hd2), (hd2, 0)):
                            sin = CT[b:b + hd2, C_SIN:C_SIN + SEQ].unsqueeze(1).to_broadcast([hd2, SPT, SEQ])
                            ins = dve.tensor_tensor(view(RS[a:a + hd2, rs], SPT), src[b:b + hd2], sin, ALU.mult)
                        ins.then_inc(taken, 1)
                        dve.wait_ge(taken, qg + (Q_G + j + 1 + 4))
                        dve.tensor_tensor(dst, RC[:, rs], RS[:, rs], ALU.add).then_inc(qk_in, 1)

                    def mask_and_max(u):
                        us, ms = slice((u % 2) * NT, (u % 2 + 1) * NT), slice((u % 2) * BPT, (u % 2 + 1) * BPT)
                        dve.wait_ge(scores, ug + (u + 1))
                        mask = CT[:, C_MASK:C_MASK + P].unsqueeze(1).to_broadcast([P, BPT, P])
                        dve.tensor_tensor(view(SM[:, us], BPT), view(SB_[u % 2], BPT), mask, ALU.add
                                          ).then_inc(s_masked, 1)
                        dve.wait_ge(s_masked, ug + (u + 1 + 2))
                        dve.tensor_reduce(MX[:, ms], view(SM[:, us], BPT), AX.X, ALU.max).then_inc(max_in, 1)
                        dve.wait_ge(max_in, ug + (u + 1))
                        dve.tensor_scalar(NMX[:, ms], MX[:, ms], -SM_SCALE, None, ALU.mult).then_inc(nmax_in, 1)

                    def normalise(u):
                        us, ms = slice((u % 2) * NT, (u % 2 + 1) * NT), slice((u % 2) * BPT, (u % 2 + 1) * BPT)
                        dve.wait_ge(exp_in, ug + (u + 1))
                        dve.reciprocal(RCP[:, ms], SUM[:, ms]).then_inc(rcp_in, 1)
                        dve.wait_ge(rcp_in, ug + (u + 1))
                        dve.tensor_tensor(view(SM[:, us], BPT), view(SM[:, us], BPT),
                                          RCP[:, ms].unsqueeze(2).to_broadcast([P, BPT, P]), ALU.mult
                                          ).then_inc(probs_in, 1)

                    def split_o(u):
                        hi_is(H_G + u, hg)
                        c = (u // 2) * TOK + (u % 2) * NT
                        dve.tensor_tensor(OL[:, c:c + NT], OB, OH[:].bitcast(F32)[:, c:c + NT], ALU.subtract
                                          ).then_inc(o_split, 1)

                    for j in range(12):
                        if j >= 6:
                            normalise(j - 6)
                        if j >= 8:
                            split_o(j - 8)
                        if j < 2:
                            rotate(j, K[:, j * NT:(j + 1) * NT])
                        elif j < 4:
                            is_prod(Q_G + j, qg)
                            if j == TT + 1:
                                dve.wait_ge(tb_done, kg + 1)
                            dve.tensor_copy(VT[:], PJ[(Q_G + j) % 4][:]).then_inc(taken, 1)
                        else:
                            u = j - 4
                            rotate(j, Q[:, (u % 2) * NT:(u % 2 + 1) * NT])
                        if j >= 5:
                            mask_and_max(j - 5)
                    after = {3: [(mask_and_max, 7)], 5: [(normalise, 7), (split_o, 5)], 9: [(split_o, 6)],
                             13: [(split_o, 7)]}
                    normalise(6)
                    split_o(4)
                    for i in range(32):
                        hh, oc, o4, t = i // 16, i // 8 % 2, i // 2 % 4, i % 2
                        q = Q_G + 12 + i
                        is_prod(q, qg)
                        if i % 16 == 0:
                            dve.wait_ge(taken, qg + (q + 4))
                        xs = slice((oc * 4 + o4) * TOK + t * NT, (oc * 4 + o4) * TOK + (t + 1) * NT)
                        dve.tensor_tensor(X1[:, xs], PJ[q % 4][:], X1[:, xs], ALU.add).then_inc(taken, 1)
                        for f, u in after.get(i, ()):
                            f(u)

                dve.wait_ge(taken, q_base + (Q_L2 + 4))
                dve.wait_ge(turned, t_base + (T_R2 + 1 + 2))
                dve.tensor_copy(R2T[:], TP[0][:, 0:KC * E2]).then_inc(split_t, 1)
                dve.wait_ge(turned, t_base + (T_B2 + 1 + 2))
                dve.tensor_copy(B2T[:], TP[1][:]).then_inc(split_t, 1)
                for t in range(TT):
                    for k in range(KC):
                        xs = slice(k * TOK + t * NT, k * TOK + (t + 1) * NT)
                        hi_is(H_X1 + t * KC + k)
                        dve.tensor_tensor(XL[:, xs], X1[:, xs], XH[:].bitcast(F32)[:, xs], ALU.subtract
                                          ).then_inc(x1_lo, 1)
                for t in range(TT):
                    is_prod(Q_L2 + t)
                    dve.tensor_copy(GT[0:E2, t * NT:(t + 1) * NT], PJ[(Q_L2 + t) % 4][0:E2, :]).then_inc(taken, 1)
                hi_is(H_A2)
                w_lo(0)
                for t in range(TT):
                    is_prod(Q_LT2 + t)
                    c = BPT * E2
                    dve.tensor_tensor(LG[:, t * c:(t + 1) * c], PJ[(Q_LT2 + t) % 4][:, 0:c],
                                      LB[:, bass.ds(hf * (TT * c) + t * c, c)], ALU.add).then_inc(taken, 1)
                dve.wait_ge(taken, q_base + (Q_LT2 + TT + 4))

                def sc(i):
                    return SC[:, i * TB:(i + 1) * TB]

                def top8(src, e):
                    hold(dve)
                    for b in range(TB):
                        ins = dve.max(M8[:, b * 8:(b + 1) * 8], src[:, b * e:(b + 1) * e])
                    chain(s_base, ins)

                def top8_index(src, e):
                    hold(dve)
                    for b in range(TB):
                        ins = dve.max_index(I8[:, b * 8:(b + 1) * 8], M8[:, b * 8:(b + 1) * 8],
                                            src[:, b * e:(b + 1) * e])
                    chain(s_base, ins)
                    chain(s_base, dve.tensor_copy(I8F[:], I8[:]))

                m8 = view(M8[:], TB)
                best = [m8[:, :, i] for i in range(2)]

                def gates(e):
                    i3 = iota[:, 0:e].unsqueeze(1).to_broadcast([P, TB, e])
                    ga, pr = view(GA[:, 0:TB * e], TB), view(PR[:, 0:TB * e], TB)
                    for i, dst in enumerate((ga, pr)):
                        idx = view(I8F[:], TB)[:, :, i:i + 1].to_broadcast([P, TB, e])
                        chain(s_base, dve.tensor_tensor(dst, i3, idx, ALU.is_equal))
                        chain(s_base, dve.tensor_tensor(dst, dst, sc(4 + i).unsqueeze(2).to_broadcast([P, TB, e]),
                                                        ALU.mult))
                    dve.tensor_tensor(ga, ga, pr, ALU.add).then_inc(gates_in_sb, 1)

                top8(LG, E2)
                top8_index(LG, E2)
                dve.tensor_tensor(sc(0), best[1], best[0], ALU.subtract).then_inc(logits_in, 1)
                dve.wait_ge(rexp, hf * 2 + 1)
                chain(s_base, dve.tensor_scalar(sc(2), sc(1), 1.0, None, ALU.add))
                chain(s_base, dve.reciprocal(sc(3), sc(2)))
                chain(s_base, dve.tensor_scalar(sc(4), sc(3), LORA_SCALE, None, ALU.mult))
                chain(s_base, dve.scalar_tensor_tensor(out=sc(5), in0=sc(1), scalar=LORA_SCALE, in1=sc(3),
                                                       op0=ALU.mult, op1=ALU.mult))
                gates(E2)
                for t in range(TT):
                    is_prod(Q_H2 + t)
                    dve.tensor_copy(H2[:, t * NT:(t + 1) * NT], PJ[(Q_H2 + t) % 4][:]).then_inc(taken, 1)

                def take_gates(q, e):
                    for t in range(TT):
                        is_prod(q + t)
                        dve.tensor_copy(GT[0:e, t * NT:(t + 1) * NT], PJ[(q + t) % 4][0:e, :]).then_inc(taken, 1)

                take_gates(Q_GT2, E2)
                hi_is(H_W2)
                w_lo(1)
                dve.wait_ge(taken, q_base + (Q_GT2 + TT + 4))
                dve.wait_ge(gates_in[0], hf * GATES_N[0] + 16 * E2)
                dve.tensor_tensor(H2[:], H2[:], GT[:], ALU.mult).then_inc(hm2_in, 1)

                def w2_block(s, i, hb, qb, last=False):
                    n = H_W2 + 1 + 3 * s
                    hi_is(n, hb)
                    w_lo(s, RF + EF if last else P)
                    for t in range(TT):
                        c_lo(i, s, t, n + 1 + t, Q_Y + 2 * s + t, qb, hb, None)

                with dve.Fori(0, KC // 2 - 1) as i:
                    bases = dve.snap(h_base + i * 6), dve.snap(q_base + i * 4)
                    for s in range(2):
                        w2_block(s, i, *bases)
                i = KC // 2 - 1
                bases = dve.snap(h_base + i * 6), dve.snap(q_base + i * 4)
                for s in range(2):
                    w2_block(s, i, *bases, last=(s == 1))

                hi_is(H_F)
                w_lo(0)
                m = RF + EF
                for t in range(TT):
                    is_prod(Q_AF + t)
                    dve.wait_ge(hf_in, hf * TT + (t + 1))
                    dve.tensor_copy(AF32[0:m, t * NT:(t + 1) * NT], PJ[(Q_AF + t) % 4][0:m, :]).then_inc(taken, 1)
                for t in range(TT):
                    is_prod(Q_LTF + t)
                    dve.tensor_copy(view(LG[:, t * BPT * EF:(t + 1) * BPT * EF], BPT),
                                    view(PJ[(Q_LTF + t) % 4][:, 0:BPT * m], BPT, RF, m)).then_inc(taken, 1)
                dve.wait_ge(taken, q_base + (Q_LTF + TT + 4))
                top8(LG, EF)
                pr3 = view(PR[:], TB)
                dve.tensor_tensor(pr3, view(LG[:], TB), m8[:, :, 0:1].to_broadcast([P, TB, EF]), ALU.subtract
                                  ).then_inc(logits_in, 1)
                dve.wait_ge(rexp, hf * 2 + 2)
                chain(s_base, dve.tensor_reduce(sc(0), pr3, AX.X, ALU.add))
                chain(s_base, dve.reciprocal(sc(1), sc(0)))
                chain(s_base, dve.tensor_tensor(pr3, pr3, sc(1).unsqueeze(2).to_broadcast([P, TB, EF]), ALU.mult))
                top8(PR, EF)
                top8_index(PR, EF)
                chain(s_base, dve.tensor_tensor(sc(2), best[0], best[1], ALU.add))
                chain(s_base, dve.tensor_scalar(sc(2), sc(2), 1e-6, None, ALU.add))
                chain(s_base, dve.reciprocal(sc(3), sc(2)))
                for i in range(2):
                    chain(s_base, dve.scalar_tensor_tensor(out=sc(4 + i), in0=best[i], scalar=FFN_SCALE, in1=sc(3),
                                                           op0=ALU.mult, op1=ALU.mult))
                gates(EF)
                hi_is(H_F + 1)
                w_lo(1)
                take_gates(Q_GTF, EF)
                for c in range(KC):
                    hi_is(H_F + 2 + c)
                    cs = slice(c * TOK, (c + 1) * TOK)
                    dve.tensor_tensor(XL[:, cs], CB[c % 2][:], XH[:].bitcast(F32)[:, cs], ALU.subtract
                                      ).then_inc(g_split, 1)
                hi_is(H_F + 10)
                w_lo(0)

                def finish(o, q, qb):
                    for t in range(TT):
                        is_prod(q + t, qb)
                        dve.scalar_tensor_tensor(out=OT[t][:], in0=PJ[(q + t) % 4][:], scalar=BFC[:, bass.ds(o, 1)],
                                                 in1=X1[:, bass.ds(o * TOK + t * NT, NT)], op0=ALU.add, op1=ALU.add
                                                 ).then_inc(taken, 1)

                def take_out(o, q, qb):
                    for t in range(TT):
                        is_prod(q + t, qb)
                        dve.wait_ge(out_done[t], (hf * KC + o) * 16 + 16)
                        dve.tensor_copy(OS[t][:], PJ[(q + t) % 4][:]).then_inc(taken, 1)

                finish(0, Q_O, q_base)

                def ffn_block(o, hb, qb, last=False):
                    hi_is(H_F + 9, hb)
                    w_lo(1)
                    if not last:
                        hi_is(H_F + 10, hb)
                        w_lo(0)
                    take_out(o - 1, Q_O - 2, qb)
                    finish(o, Q_O, qb)

                with dve.Fori(1, KC - 1) as o:
                    ffn_block(o, dve.snap(h_base + o * 2), dve.snap(q_base + o * 4))
                o = KC - 1
                ffn_block(o, dve.snap(h_base + o * 2), dve.snap(q_base + o * 4), last=True)
                take_out(KC - 1, Q_O + 4 * KC - 2, q_base)
                assert steps[0] == STEP_N, steps[0]


def kernel(x, itok_B_0_23, itok_B_0_7, L0_cond_W, L0_cond_b, L0_cond_lora_As, L0_cond_lora_Bs, L0_attn_wq,
           L0_attn_wk, L0_attn_wv, L0_attn_wo, L0_cond2_W, L0_cond2_Wr, L0_cond2_A, L0_cond2_B, L0_ffn_base_w,
           L0_ffn_base_b, L0_ffn_A, L0_ffn_B, L0_ffn_router_w):
    import concourse.bacc as bacc
    from concourse.bass_utils import run_bass_kernel_spmd

    host = {
        "x": np.asarray(x).reshape(BATCH * SEQ, D),
        "ids1": np.asarray(itok_B_0_23),
        "ids2": np.asarray(itok_B_0_7).reshape(BATCH // 2, 2).T,
        "W1": np.asarray(L0_cond_W),
        "b1": np.asarray(L0_cond_b).reshape(KC, P).T,
        "A1": np.asarray(L0_cond_lora_As).reshape(SLOTS * D, RANK1),
        "B1": np.asarray(L0_cond_lora_Bs).reshape(SLOTS * RANK1, D),
        "wq": np.asarray(L0_attn_wq),
        "wk": np.asarray(L0_attn_wk),
        "wv": np.asarray(L0_attn_wv),
        "wo": np.asarray(L0_attn_wo),
        "W2": np.asarray(L0_cond2_W),
        "Wr2": np.asarray(L0_cond2_Wr),
        "A2": np.asarray(L0_cond2_A).reshape(E2 * R2, D),
        "B2": np.asarray(L0_cond2_B),
        "Wf": np.asarray(L0_ffn_base_w),
        "bf": np.asarray(L0_ffn_base_b).reshape(KC, P).T,
        "Af": np.asarray(L0_ffn_A),
        "Bf": np.asarray(L0_ffn_B),
        "Rf": np.asarray(L0_ffn_router_w),
        "consts": constants(),
    }
    nc = bacc.Bacc("TRN2", target_bir_lowering=False, num_devices=1)
    arrays, args = {}, {}
    for name, a in host.items():
        a = np.ascontiguousarray(a)
        arrays[f"in_{name}"] = a
        args[name] = nc.dram_tensor(f"in_{name}", a.shape, mybir.dt.from_np(a.dtype), kind="ExternalInput").ap()
    args["scratch"] = nc.dram_tensor("gates_scratch", (E2 + EF, TOK), F32, kind="Internal").ap()
    args["out"] = nc.dram_tensor("out_0", (BATCH * SEQ, D), F32, kind="ExternalOutput").ap()
    build(nc, **args)
    r = run_bass_kernel_spmd(nc, [arrays], core_ids=[0])
    return r.results[0]["out_0"].reshape(BATCH, SEQ, D)
```

```python
from contextlib import ExitStack

import numpy as np

import concourse.bass as bass
from concourse import mybir

F32 = mybir.dt.float32
F32R = mybir.dt.float32r
I32 = mybir.dt.int32
U32 = mybir.dt.uint32
ALU = mybir.AluOpType
ACT = mybir.ActivationFunctionType
AX = mybir.AxisListType

P = 128
D = 1024
KC = D // P
SEQ = 64
BATCH = 32
HALVES = 2
TOK = BATCH * SEQ // HALVES
NT = 512
TT = TOK // NT
TB = TOK // P
BPT = NT // P
HD = 128
NKV = 8
GQ = 4
RANK1 = 16
SLOTS = 32
SPT = NT // SEQ
E2, R2 = 8, 16
EF, RF = 16, 64
SM_SCALE = float(HD) ** -0.5
LORA_SCALE = 2.0
FFN_SCALE = 0.5
LANG_BIAS = 5.0
MASKED = -3.0e38

C_ID, C_MASK, C_COS, C_SIN, C_LORA, C_IOTA = 0, 128, 256, 320, 384, 392
C_COLS = 408


def constants():
    t = np.zeros((P, C_COLS), np.float32)
    t[:, C_ID:C_ID + P] = np.eye(P, dtype=np.float32)
    tok = np.arange(P)
    same = tok[:, None] // SEQ == tok[None, :] // SEQ
    t[:, C_MASK:C_MASK + P] = np.where(same & (tok[None, :] <= tok[:, None]), 0.0, MASKED)
    half = HD // 2
    inv_freq = (np.float32(10000.0) ** (-np.arange(half, dtype=np.float32) / np.float32(half))).astype(np.float32)
    ang = np.arange(SEQ, dtype=np.float32)[None, :] * inv_freq[:, None]
    t[:, C_COS:C_COS + SEQ] = np.tile(np.cos(ang), (2, 1))
    t[:half, C_SIN:C_SIN + SEQ] = np.sin(ang)
    t[half:, C_SIN:C_SIN + SEQ] = -np.sin(ang)
    t[:, C_LORA:C_LORA + SPT] = LORA_SCALE * (tok[:, None] // RANK1 == np.arange(SPT)[None, :])
    t[:, C_IOTA:C_IOTA + EF] = np.arange(EF)[None, :]
    return t


PER_G = 10
D_N = PER_G * NKV
RAW_W, RAW_D = 0, KC
RAW_A2 = RAW_D + D_N
RAW_M, RAW_B = RAW_A2 + 1, RAW_A2 + 1 + KC
RAW_N = RAW_B + KC
T_W0, T_X, T_W, T_A2, T_B = 0, 1, TB, TB + KC, TB + KC + 1
T_N = T_B + KC
M_AF, M_AR = RF + EF, RF + EF + E2

Q_H, Q_C = 0, TT
Q_G = Q_C + TT * KC
Q_PER_G = 12 + 32
Q_3 = Q_G + Q_PER_G * NKV
STAGE3 = ("ar0 ar1 h0 lt0 lt1 h1 m00 m01 gt0 gt1 m10 m11 m20 bh0 bh1 m21 lf0 lf1 m30 m31 gf0 gf1 "
          "m40 m41 m50 m51 m60 m61 m70 m71").split()
Q3 = {n: Q_3 + i for i, n in enumerate(STAGE3)}
Q_O = Q_3 + len(STAGE3)
Q_N = Q_O + 4 * KC

H_W, H_X, H_A, H_C = 0, 1, TB + 1, TB + 2
H_G = H_C + 3 * KC - 1
H_X1 = H_G + 8 * NKV
H3 = {n: H_X1 + TT * KC + i for i, n in enumerate("a2 m0 m1 m2 m3 m4 m5 m6 g0 g1 g2 m7 g3 g4 g5 g6 b0 g7".split())}
H_B = H_X1 + TT * KC + len(H3)
HI_N = H_B + KC - 1
SPLIT_D = D_N + 1
STEP_N = 27


def raw_count(r):
    return 16 * (r // 2 + 1)


RAW_GAIN = [raw_count(RAW_N - 1 - (RAW_N - 1 - s) % 2) for s in range(2)]


def build(nc, x, ids1, ids2, W1, b1, A1, B1, wq, wk, wv, wo, W2, Wr2, A2, B2, Wf, bf, Af, Bf, Rf, consts,
          gates_d, m_d, c2_d, out):
    assert D == TOK and KC == TB
    with ExitStack() as ctx:
        at = [0]
        BASE = (nc.sbuf_base + 31) // 32 * 32

        def sb(name, shape, dt=F32, offset=None):
            size = 4 * int(np.prod(shape[1:]))
            if offset is None:
                offset = at[0]
                at[0] += (size + 31) // 32 * 32
            return nc.alloc_sbuf_tensor_at(name, shape, dt, offset=BASE + offset)

        KB = 1024
        CH = sb("c_hi", [P, KC * TOK], F32R)
        CL = sb("c_lo", [P, KC * TOK], F32R)
        XR = sb("x_raw", [P, TB * D], offset=0)
        AH = sb("lora_a_hi", [P, TT * D], F32R, offset=24 * KB)
        AL = sb("lora_a_lo", [P, TT * D], F32R, offset=48 * KB)
        AW = sb("lora_a_raw", [P, TT * D], offset=56 * KB)
        MT = sb("m_rows", [P, 4 * D], offset=32 * KB)
        ER = sb("small_raw", [P, D], offset=52 * KB)
        XH = sb("x_hi", [P, KC * TOK], F32R)
        XL = sb("x_lo", [P, KC * TOK], F32R)
        OH = sb("o_hi", [P, GQ * TOK], F32R, offset=64 * KB)
        OL = sb("o_lo", [P, GQ * TOK], F32R, offset=80 * KB)
        K = sb("k_rot", [P, TOK], offset=96 * KB)
        V = sb("v_tok", [P, TB * HD], offset=100 * KB)
        VT = sb("v_feat", [P, NT], offset=104 * KB)
        Q = sb("q_rot", [P, 2 * NT], offset=106 * KB)
        SM = sb("probs", [P, 2 * NT], offset=110 * KB)
        PT = sb("probs_t", [P, 2 * NT], offset=114 * KB)
        RC = sb("rope_cos", [P, 2 * NT], offset=118 * KB)
        RS = sb("rope_sin", [P, 2 * NT], offset=122 * KB)
        NMX = sb("neg_max", [P, 2 * BPT], offset=126 * KB)
        MX = sb("row_max", [P, 2 * BPT], offset=126 * KB + 64)
        SUM = sb("row_sum", [P, 2 * BPT], offset=126 * KB + 128)
        RCP = sb("row_rcp", [P, 2 * BPT], offset=126 * KB + 192)
        AF32 = sb("small_out", [P, TOK], offset=64 * KB)
        G32 = sb("g_f32", [P, KC * TOK], offset=96 * KB)
        X1 = sb("x1", [P, KC * TOK])
        RAW = [sb(f"raw{i}", [P, D]) for i in range(2)]
        WH = [sb(f"w_hi{i}", [P, D], F32R) for i in range(2)]
        WL = [sb(f"w_lo{i}", [P, D], F32R) for i in range(2)]
        buf = at[0]
        at[0] += 12 * KB
        ES = sb("small_t", [P, KC * M_AF], offset=buf)
        B1S = sb("b1_rows", [P, TT * D], offset=buf)
        HM = sb("h_masked", [P, TT * NT], offset=buf + 8 * KB)
        HF = sb("h_twice", [P, TOK], offset=buf)
        GT = sb("gates_t", [P, TOK], offset=buf + 4 * KB)
        H2 = sb("h2", [P, TOK], offset=buf + 8 * KB)
        OT = [sb(f"out_t{t}", [P, NT], offset=buf + 2 * KB * t) for t in range(TT)]
        OS = [sb(f"out_s{t}", [P, NT], offset=buf + (4 + 2 * t) * KB) for t in range(TT)]
        BC = [sb(f"lora_b{i}", [P, TT * P]) for i in range(2)]
        CT = sb("consts_sb", [P, C_COLS])
        B1C = sb("bias1", [P, KC])
        BFC = sb("biasf", [P, KC])
        ID1 = sb("ids1_sb", [1, BATCH], I32)
        LID = sb("lang_id", [P, HALVES * TB], I32)
        LIDF = sb("lang_idf", [P, HALVES * TB])
        LB = sb("lang_bias", [P, HALVES * TB * E2])
        AR32 = sb("small_folded", [P, KC * M_AR])
        BA32 = sb("small_b2", [P, M_AF])
        LG = sb("logits", [P, TB * EF])
        PR = sb("route_p", [P, TB * EF])
        GA = sb("gate_a", [P, TB * EF])
        M8 = sb("top8", [P, TB * 8])
        I8 = sb("top8_i", [P, TB * 8], U32)
        I8F = sb("top8_f", [P, TB * 8])
        SC = sb("route_s", [P, 6 * TB])
        assert BASE + at[0] <= nc.SBUF_PARTITION_SIZE_BYTES, at[0]

        PJ = [ctx.enter_context(nc.psum_tensor(f"prod{i}", [P, NT], F32)) for i in range(4)]
        TP = [ctx.enter_context(nc.psum_tensor(f"turned{i}", [P, D], F32)) for i in range(2)]
        SB_ = [TP[0][:, i * NT:(i + 1) * NT] for i in range(2)]
        TBK = TP[1][:, 0:NT]
        OB = TP[1][:, NT:2 * NT]

        def sem(name):
            return ctx.enter_context(nc.semaphore(name))

        ident_in = sem("ident_in")
        const_in = sem("const_in")
        wf_in = [sem(f"wf_in{b}") for b in range(KC)]
        small_in = sem("small_in")
        fold_in = [sem("fold_in0"), sem("fold_in1")]
        fold_turned = sem("fold_turned")
        fold_hi = sem("fold_hi")
        fold_split = sem("fold_split")
        fold_w = sem("fold_w")
        fold_prod = sem("fold_prod")
        fold_taken = sem("fold_taken")
        m_out = [sem(f"m_out{i}") for i in range(4)]
        x_in = [sem(f"x_in{b}") for b in range(TB)]
        a_in = sem("a_in")
        raw_in = [sem("raw_in0"), sem("raw_in1")]
        b1_in = sem("b1_in")
        c2_in = [sem("c2_in0"), sem("c2_in1")]
        gates_out = sem("gates_out")
        gates_in = sem("gates_in")
        comb_in = [sem(f"comb_in{i}") for i in range(KC // 2)]
        out_done = [sem("out_done0"), sem("out_done1")]
        turned = sem("turned")
        split_t = sem("split_t")
        wd_hi = sem("wd_hi")
        split_d = sem("split_d")
        split_m = sem("split_m")
        a_split = sem("a_split")
        hi_done = sem("hi_done")
        prod = sem("prod")
        taken = sem("taken")
        bc_in = sem("bc_in")
        x_res = sem("x_res")
        qk_in = sem("qk_in")
        scores = sem("scores")
        s_masked = sem("s_masked")
        max_in = sem("max_in")
        nmax_in = sem("nmax_in")
        exp_in = sem("exp_in")
        rcp_in = sem("rcp_in")
        probs_in = sem("probs_in")
        tb_done = sem("tb_done")
        tb_taken = sem("tb_taken")
        pv_done = sem("pv_done")
        o_split = sem("o_split")
        x1_lo = sem("x1_lo")
        step = sem("dve_step")
        logits_in = sem("logits_in")
        rexp = sem("route_exp")
        gates_in_sb = sem("gates_tok")
        hg_in = sem("hg_in")
        hf_in = sem("hf_in")
        g_prod = sem("g_prod")
        g_split = sem("g_split")

        held = {e.engine: sem(f"held_{n}") for n, e in (("sp", nc.sync), ("pe", nc.tensor), ("act", nc.scalar),
                                                        ("pool", nc.gpsimd), ("dve", nc.vector))}

        ident = CT[:, C_ID:C_ID + P]
        iota = CT[:, C_IOTA:C_IOTA + EF]

        block = ctx.enter_context(nc.Block())

        def view(t, n, lo=0, hi=None):
            v = t.rearrange("p (n m) -> p n m", n=n)
            return v[:, :, lo:hi] if hi is not None else v

        def hold(eng):
            eng.sem_inc(held[eng.engine], 1)

        def per_half(eng, hf):
            return (eng.snap(hf * Q_N), eng.snap(hf * T_N))

        @block.sync
        def _(sp):
            for t in range(TT):
                sp.sem_inc(out_done[t], 16)
            sp.dma_start(CT[:], consts).then_inc(ident_in, 16)
            for src, at_row in ((Af, 0), (Rf, RF), (Wr2, M_AF)):
                sp.dma_start(ER[at_row:at_row + src.shape[0], :], src).then_inc(small_in, 16)

            def load_wf(b):
                sp.dma_start(X1[:, b * D:(b + 1) * D], Wf[b * P:(b + 1) * P, :]).then_inc(wf_in[b], 16)

            def load_w2(i):
                sp.dma_start(view(RAW[i % 2][:], KC), W2.rearrange("(k p) n -> p k n", p=P)[:, :, i * P:(i + 1) * P]
                             ).then_inc(fold_in[i % 2], 16)

            for b in range(KC // 2):
                load_wf(b)
            load_w2(0)
            for b in range(KC // 2, KC):
                load_wf(b)
            load_w2(1)
            sp.dma_start(B1C[:], b1).then_inc(const_in, 16)
            sp.dma_start(BFC[:], bf).then_inc(const_in, 16)
            sp.dma_start(ID1[:], ids1.rearrange("(a b) -> a b", a=1)).then_inc(const_in, 16)
            for s in range(2):
                sp.dma_start(LID[s * SEQ:(s + 1) * SEQ, :],
                             ids2[s:s + 1, :].to_broadcast([SEQ, HALVES * TB])).then_inc(const_in, 16)
            for i in range(2, KC + 1):
                sp.wait_ge(fold_w, i - 1)
                sp.wait_ge(fold_prod, 3 * (i - 2) + 1)
                if i < KC:
                    load_w2(i)
                else:
                    raw_b2 = RAW[0][:].rearrange("p (c e r) -> p c e r", c=KC, e=E2)
                    for c in range(KC):
                        sp.dma_start(raw_b2[:, c], B2[:, c * P:(c + 1) * P, :].rearrange("e p r -> p e r")
                                     ).then_inc(fold_in[0], 16)
            sp.wait_ge(const_in, 16 * 5)
            hold(sp)

            with sp.Fori(0, HALVES) as hf:
                q_base, t_base = per_half(sp, hf)
                d_base = sp.snap(hf * SPLIT_D)
                m_base = sp.snap(hf * KC)

                def load(s, src, dst=None):
                    sp.dma_start(RAW[s][:] if dst is None else dst, src).then_inc(raw_in[s], 16)

                def adapter(n):
                    return sp.value_load(ID1[0:1, bass.ds(hf * (BATCH // HALVES) + n, 1)],
                                         min_val=0, max_val=SLOTS - 1)

                sp.wait_ge(turned, t_base + (-1 + 2))
                hold(sp)
                for b in range(TB):
                    sp.dma_start(XR[:, b * D:(b + 1) * D], x[bass.ds(hf * TOK + b * P, P), :]).then_inc(x_in[b], 16)
                for n in range(TT * SPT):
                    t, n8 = n // SPT, n % SPT
                    m = adapter(n)
                    sp.dma_start(view(AW[:, t * D:(t + 1) * D], KC, n8 * RANK1, (n8 + 1) * RANK1),
                                 A1[bass.ds(m * D, D), :].rearrange("(k p) r -> p k r", p=P)).then_inc(a_in, 16)
                sp.wait_ge(fold_w, KC + 1)
                sp.wait_ge(fold_prod, 3 * KC + 1)
                sp.wait_ge(turned, t_base + 2)
                hold(sp)
                for j in range(2):
                    load(j, W1[j * P:(j + 1) * P, :])
                for t in range(TT):
                    sp.wait_ge(out_done[t], hf * (16 * KC) + 16)
                sp.wait_ge(fold_prod, 3 * (KC + 1))
                hold(sp)
                for n in range(TT * SPT):
                    t, n8 = n // SPT, n % SPT
                    m = adapter(n)
                    sp.dma_start(B1S[n8 * RANK1:(n8 + 1) * RANK1, t * D:(t + 1) * D],
                                 B1[bass.ds(m * RANK1, RANK1), :]).then_inc(b1_in, 16)
                with sp.Fori(1, KC // 2) as i:
                    for s in range(2):
                        sp.wait_ge(turned, t_base + i * 2 + (T_W + s - 1 + 2))
                        load(s, W1[bass.ds(i * (2 * P) + s * P, P), :])
                sp.wait_ge(turned, t_base + (T_W + KC + 2))
                hold(sp)
                with sp.Fori(0, NKV) as g:
                    dg = sp.snap(d_base + g * PER_G)

                    def col(w, c):
                        return w.rearrange("(k p) n -> p k n", p=P)[:, :, bass.ds(c, P)]

                    srcs = [col(wk, g * P), col(wv, g * P)]
                    srcs += [col(wq, g * (GQ * P) + h * P) for h in range(GQ)]
                    for hh in range(2):
                        for oc in range(2):
                            srcs.append(wo[bass.ds(g * (GQ * HD) + hh * 2 * HD, 2 * HD),
                                           oc * NT:(oc + 1) * NT].rearrange("(h d) n -> d h n", d=HD))
                    for j, src in enumerate(srcs):
                        sp.wait_ge(split_d, dg + (j - 1 + 2))
                        load(j % 2, src, view(RAW[j % 2][:], 2 if j >= 6 else KC))
                sp.wait_ge(split_d, d_base + (D_N + 2))
                load(RAW_A2 % 2, A2)
                for i in range(4):
                    sp.wait_ge(m_out[i], 16 * (KC // 4 + (i == 0)))

                def load_m(j):
                    if j == 1:
                        sp.wait_ge(turned, t_base + (T_A2 + 1 + 2))
                    if j >= 2:
                        sp.wait_ge(split_m, m_base + (j - 2 + 1))
                    load((RAW_M + j) % 2, m_d[j])

                for j in range(4):
                    load_m(j)
                sp.wait_ge(taken, q_base + (Q3["gt1"] + 1 + 4))
                sp.dma_start(gates_d[0:E2, :], GT[0:E2, :]).then_inc(gates_out, 16)
                sp.wait_ge(gates_out, hf * 32 + 16)
                for e in range(E2):
                    sp.dma_start(GT[e * R2:(e + 1) * R2, :], gates_d[e:e + 1, :].to_broadcast([R2, TOK])
                                 ).then_inc(gates_in, 16)
                for j in range(4, 7):
                    load_m(j)
                sp.wait_ge(taken, q_base + (Q3["gf1"] + 1 + 4))
                sp.dma_start(gates_d[E2:E2 + EF, :], GT[0:EF, :]).then_inc(gates_out, 16)
                sp.wait_ge(gates_out, hf * 32 + 32)
                for e in range(EF):
                    c, row = e // 2, (e % 2) * RF
                    sp.dma_start(G32[row:row + RF, c * TOK:(c + 1) * TOK],
                                 gates_d[E2 + e:E2 + e + 1, :].to_broadcast([RF, TOK])).then_inc(comb_in[c // 2], 16)
                load_m(7)

                def load_b(s, o, c2_free=None):
                    rows = bass.ds(o, P)
                    load((RAW_B + s) % 2, Bf[:, rows, :].rearrange("e p r -> p e r"),
                         RAW[(RAW_B + s) % 2][:].rearrange("p (e r) -> p e r", e=EF))
                    if c2_free is not None:
                        sp.wait_ge(prod, c2_free)
                        hold(sp)
                    sp.dma_start(BC[s][:, 0:P], c2_d[:, rows]).then_inc(c2_in[s], 16)

                for s in range(2):
                    sp.wait_ge(split_m, m_base + (KC - 2 + s + 1))
                    load_b(s, s * P)
                with sp.Fori(1, KC // 2) as i:
                    for s in range(2):
                        sp.wait_ge(turned, t_base + i * 2 + (T_B + s - 2 + 1 + 2))
                        load_b(s, i * (2 * P) + s * P, q_base + i * 8 + (Q_O + 4 * (s - 2) + 2))
            for t in range(TT):
                sp.wait_ge(out_done[t], HALVES * KC * 16 + 16)

        @block.tensor
        def _(pe):
            pe.sem_inc(turned, 2)
            pe.wait_ge(ident_in, 16)

            def turn_block(par, raw, rows, done):
                for c in range(KC):
                    mm = pe.transpose(TP[par][:, c * P:c * P + rows], raw[0:rows, c * P:(c + 1) * P],
                                      ident[0:rows, 0:rows])
                mm.then_inc(done, 1)

            def three(dst, wh, wl, xh, xl, start, stop):
                pe.matmul(dst, wh, xh, start=start, stop=False)
                pe.matmul(dst, wh, xl, start=False, stop=False)
                return pe.matmul(dst, wl, xh, start=False, stop=stop)

            def main(q, s, t, XHi, XLo, start=True, stop=True, m=P, chunk=lambda k: None):
                for k in range(KC):
                    chunk(k)
                    xs = slice(k * TOK + t * NT, k * TOK + (t + 1) * NT)
                    ws = slice(k * P, k * P + m)
                    mm = three(PJ[q % 4][0:m, :], WH[s][:, ws], WL[s][:, ws], XHi[:, xs], XLo[:, xs],
                               start and k == 0, stop and k == KC - 1)
                return mm

            pe.wait_ge(small_in, 16 * 3)
            hold(pe)
            turn_block(0, ER, M_AR, fold_turned)

            def turn_wf(b):
                pe.wait_ge(wf_in[b], 16)
                if b >= 1:
                    pe.wait_ge(fold_split, b)
                turn_block((b + 1) % 2, X1[:, b * D:(b + 1) * D], P, fold_turned)

            def fold_bank(q):
                if q >= 4:
                    pe.wait_ge(fold_taken, q - 3)

            for b in range(KC // 2):
                turn_wf(b)
            for i in range(KC + 1):
                fold_bank(3 * i)
                pe.wait_ge(fold_in[i % 2], 16 * (i // 2 + 1) if i < KC else 16 * (KC // 2 + KC))
                if i == 0:
                    pe.wait_ge(fold_split, 1)
                for k in range(KC):
                    mm = pe.matmul(PJ[3 * i % 4][:, 0:M_AF], RAW[i % 2][:, k * P:(k + 1) * P],
                                   ES[:, k * M_AF:(k + 1) * M_AF], start=(k == 0), stop=(k == KC - 1))
                mm.then_inc(fold_prod, 1)
                pe.wait_ge(fold_w, i + 1)
                hold(pe)
                for t in range(D // NT):
                    fold_bank(3 * i + 1 + t)
                    if i == 0:
                        pe.wait_ge(fold_split, 1 + (t + 1) * (KC // 2))

                    def chunk(k):
                        if i == 0 and t == 0 and k % 2 == 1:
                            turn_wf(KC // 2 + k // 2)

                    main(3 * i + 1 + t, i % 2, t, XH, XL, chunk=chunk).then_inc(fold_prod, 1)
            pe.wait_ge(fold_taken, 3 * (KC + 1))
            hold(pe)

            with pe.Fori(0, HALVES) as hf:
                q_base, t_base = per_half(pe, hf)
                r_base = [pe.snap(hf * RAW_GAIN[s]) for s in range(2)]

                def raw_ready(r, base=None):
                    pe.wait_ge(raw_in[r % 2], (r_base if base is None else base)[r % 2] + raw_count(r))

                def turn(k, ready, raw=None, base=None):
                    ready()
                    pe.wait_ge(split_t, (t_base if base is None else base) + (k - 1 + 2))
                    turn_block(k % 2, RAW[k % 2] if raw is None else raw, P, turned)

                def bank_free(q, base=None):
                    pe.wait_ge(taken, (q_base if base is None else base) + (q + 1))

                pe.wait_ge(split_t, t_base + 2)
                hold(pe)
                turn(T_W0, lambda: raw_ready(RAW_W))

                def turn_x(b):
                    turn(T_X + b, lambda: pe.wait_ge(x_in[b], hf * 16 + 16), raw=XR[:, b * D:(b + 1) * D])

                for b in range(BPT + 1):
                    turn_x(b)

                def b1_part(s, t, first):
                    pe.matmul(PJ[(first + t) % 4][:], BC[s][:, t * P:(t + 1) * P], HM[:, t * NT:(t + 1) * NT],
                              start=False, stop=True).then_inc(prod, 1)

                def w1_block0(bcb):
                    for t in range(TT):
                        pe.wait_ge(split_t, t_base + (T_X + (t + 1) * BPT - 1 + 1 + 2))
                        hold(pe)
                        bank_free(Q_C + t)

                        def chunk(k):
                            if t == 0 and k in (1, 3, 5):
                                turn_x(BPT + (k + 1) // 2)

                        main(Q_C + t, 0, t, XH, XL, stop=False, chunk=chunk)
                    pe.wait_ge(a_split, hf + 1)
                    hold(pe)
                    for t in range(TT):
                        bank_free(Q_H + t)
                        for k in range(KC):
                            xs = slice(k * TOK + t * NT, k * TOK + (t + 1) * NT)
                            ws = slice(t * D + k * P, t * D + (k + 1) * P)
                            mm = three(PJ[(Q_H + t) % 4][:], AH[:, ws], AL[:, ws], XH[:, xs], XL[:, xs],
                                       k == 0, k == KC - 1)
                        mm.then_inc(prod, 1)
                    turn(T_W + 1, lambda: raw_ready(RAW_W + 1))
                    pe.wait_ge(taken, q_base + (Q_H + TT + 4))
                    pe.wait_ge(bc_in, bcb + 1)
                    hold(pe)
                    for t in range(TT):
                        b1_part(0, t, Q_C)

                def w1_block(s, tb, rb, qb, bcb, last=False):
                    if not last:
                        turn(T_W + s + 1, lambda: raw_ready(RAW_W + s + 1, rb), base=tb)
                    pe.wait_ge(split_t, tb + (T_W + s + 1 + 2))
                    pe.wait_ge(bc_in, bcb + (s + 1))
                    hold(pe)
                    for t in range(TT):
                        bank_free(Q_C + 2 * s + t, qb)
                        main(Q_C + 2 * s + t, s, t, XH, XL, stop=False)
                        b1_part(s, t, Q_C + 2 * s)

                def w1_bases(i):
                    return (pe.snap(t_base + i * 2), [pe.snap(r_base[s] + i * 16) for s in range(2)],
                            pe.snap(q_base + i * 4), pe.snap(hf * KC + i * 2))

                bases = w1_bases(0)
                w1_block0(bases[-1])
                w1_block(1, *bases)
                with pe.Fori(1, KC // 2 - 1) as i:
                    bases = w1_bases(i)
                    for s in range(2):
                        w1_block(s, *bases)
                bases = w1_bases(KC // 2 - 1)
                for s in range(2):
                    w1_block(s, *bases, last=(s == 1))

                pe.wait_ge(taken, q_base + (Q_G - 1 + 4))
                hold(pe)
                with pe.Fori(0, NKV) as g:
                    qg = pe.snap(q_base + g * Q_PER_G)
                    dg = pe.snap(hf * SPLIT_D + g * PER_G)
                    ug = pe.snap(hf * (NKV * 8) + g * 8)
                    kg = pe.snap(hf * (NKV * 10) + g * 10)

                    def turn_v(t):
                        pe.wait_ge(taken, qg + (Q_G + TT + t + 1 + 4))
                        pe.wait_ge(tb_taken, kg + (t + 1))
                        for b in range(BPT):
                            mm = pe.transpose(TBK[:, b * P:(b + 1) * P], VT[:, b * P:(b + 1) * P], ident)
                        mm.then_inc(tb_done, 1)

                    def score(u):
                        pe.wait_ge(qk_in, kg + (TT + u + 1))
                        pe.wait_ge(s_masked, ug + (u + 1))
                        t = u % TT
                        for b in range(BPT):
                            mm = pe.matmul(SB_[u % 2][:, b * P:(b + 1) * P],
                                           Q[:, (u % 2) * NT + b * P:(u % 2) * NT + (b + 1) * P],
                                           K[:, t * NT + b * P:t * NT + (b + 1) * P], start=True, stop=True)
                        mm.then_inc(scores, 1)

                    def turn_p(u):
                        pe.wait_ge(probs_in, ug + (u + 1))
                        pe.wait_ge(tb_taken, kg + (TT + u + 1))
                        for b in range(BPT):
                            c = (u % 2) * NT + b * P
                            mm = pe.transpose(TBK[:, b * P:(b + 1) * P], SM[:, c:c + P], ident)
                        mm.then_inc(tb_done, 1)

                    def pv(u):
                        pe.wait_ge(tb_taken, kg + (TT + u + 1 + 1))
                        pe.wait_ge(o_split, ug + (u + 1))
                        t = u % TT
                        for b in range(BPT):
                            c = (u % 2) * NT + b * P
                            mm = pe.matmul(OB[:, b * P:(b + 1) * P], V[:, (t * BPT + b) * HD:(t * BPT + b + 1) * HD],
                                           PT[:, c:c + P], start=True, stop=True)
                        mm.then_inc(pv_done, 1)

                    def attention(j):
                        if 0 <= j - 5 < 8:
                            score(j - 5)
                        if 0 <= j - 6 < 8:
                            turn_p(j - 6)
                        if 0 <= j - 7 < 8:
                            pv(j - 7)

                    for j in range(12):
                        if j % TT == 0:
                            pe.wait_ge(split_d, dg + (j // TT + 1 + 2))
                        if j == 1:
                            pe.wait_ge(taken, q_base + (Q_G + 4))
                            hold(pe)
                        bank_free(Q_G + j, qg)
                        main(Q_G + j, (j // TT) % 2, j % TT, CH, CL).then_inc(prod, 1)
                        if j in (3, 4):
                            turn_v(j - 3)
                        attention(j)
                    for i in range(32):
                        hh, oc, o4, t = i // 16, i // 8 % 2, i // 2 % 4, i % 2
                        if i % 8 == 0:
                            pe.wait_ge(split_d, dg + (6 + i // 8 + 1 + 2))
                        if i % 16 == 0:
                            pe.wait_ge(o_split, ug + (4 * (hh + 1) + 1))
                        q = Q_G + 12 + i
                        bank_free(q, qg)
                        s = (i // 8) % 2
                        for h2 in range(2):
                            ws = slice(h2 * NT + o4 * P, h2 * NT + (o4 + 1) * P)
                            xs = slice((2 * hh + h2) * TOK + t * NT, (2 * hh + h2) * TOK + (t + 1) * NT)
                            mm = three(PJ[q % 4][:], WH[s][:, ws], WL[s][:, ws], OH[:, xs], OL[:, xs],
                                       h2 == 0, h2 == 1)
                        mm.then_inc(prod, 1)
                        if i in (3, 7, 11):
                            attention(12 + i // 4)

                turn(T_A2, lambda: raw_ready(RAW_A2))
                m_base = pe.snap(hf * KC)
                x_base = pe.snap(hf * (TT * KC))
                pe.wait_ge(split_d, hf * SPLIT_D + (SPLIT_D + 2))
                hold(pe)

                def x1_chunk(t):
                    def ready(k):
                        pe.wait_ge(x1_lo, x_base + (t * KC + k + 1))
                    return ready

                def small(t):
                    q = Q3[f"ar{t}"]
                    bank_free(q)
                    main(q, 0, t, CH, CL, m=M_AR, chunk=x1_chunk(t)).then_inc(prod, 1)

                def h2(t):
                    q = Q3[f"h{t}"]
                    bank_free(q)
                    main(q, 1, t, CH, CL).then_inc(prod, 1)

                def by_token(name, source, m):
                    for t in range(TT):
                        q = Q3[f"{name}{t}"]
                        pe.wait_ge(taken, q_base + (Q3[f"{source}{t}"] + 1 + 4))
                        hold(pe)
                        bank_free(q)
                        for b in range(BPT):
                            mm = pe.transpose(PJ[q % 4][:, b * m:(b + 1) * m],
                                              AF32[0:m, t * NT + b * P:t * NT + (b + 1) * P], ident[0:m, 0:m])
                        mm.then_inc(prod, 1)

                def gates_by_expert(name, e):
                    for t in range(TT):
                        q = Q3[f"{name}{t}"]
                        bank_free(q)
                        for b in range(BPT):
                            c = (t * BPT + b) * e
                            mm = pe.transpose(PJ[q % 4][0:e, b * P:(b + 1) * P], GA[:, c:c + e], ident)
                        mm.then_inc(prod, 1)

                def m_block(j, t):
                    q = Q3[f"m{j}{t}"]
                    if t == 0:
                        pe.wait_ge(split_m, m_base + (j + 1))
                        hold(pe)
                    bank_free(q)
                    main(q, j % 2, t, CH, CL).then_inc(prod, 1)

                for t in range(TT):
                    small(t)
                pe.wait_ge(split_t, t_base + (T_A2 + 1 + 2))
                hold(pe)
                h2(0)
                by_token("lt", "ar", M_AR)
                h2(1)
                m_block(0, 0)
                m_block(0, 1)
                pe.wait_ge(gates_in_sb, hf * 2 + 1)
                hold(pe)
                gates_by_expert("gt", E2)
                m_block(1, 0)
                m_block(1, 1)
                m_block(2, 0)
                pe.wait_ge(hg_in, hf + 1)
                hold(pe)
                for t in range(TT):
                    q = Q3[f"bh{t}"]
                    bank_free(q)
                    pe.matmul(PJ[q % 4][0:M_AF, :], BA32[:], H2[:, t * NT:(t + 1) * NT], start=True, stop=True
                              ).then_inc(prod, 1)
                m_block(2, 1)
                by_token("lf", "bh", M_AF)
                m_block(3, 0)
                m_block(3, 1)
                pe.wait_ge(gates_in_sb, hf * 2 + 2)
                hold(pe)
                gates_by_expert("gf", EF)
                for j in range(4, KC):
                    if j == KC - 1:
                        turn(T_B, lambda: raw_ready(RAW_B))
                    for t in range(TT):
                        m_block(j, t)

                def turn_out(q, qb):
                    for t in range(TT):
                        pe.wait_ge(taken, qb + (q - 2 + t + 1 + 4))
                        for b in range(BPT):
                            mm = pe.transpose(PJ[(q + t) % 4][:, b * P:(b + 1) * P],
                                              OT[t][:, b * P:(b + 1) * P], ident)
                        mm.then_inc(prod, 1)

                def ffn_block(s, tb, rb, qb, cb, first=False, last=False):
                    if not last:
                        turn(T_B + s + 1, lambda: raw_ready(RAW_B + s + 1, rb), base=tb)
                    pe.wait_ge(split_t, tb + (T_B + s + 1 + 2))
                    hold(pe)
                    for t in range(TT):
                        q = Q_O + 4 * s + t
                        bank_free(q, qb)

                        def chunk(k):
                            if first and t == 0:
                                pe.wait_ge(g_split, hf * KC + (k + 1))

                        main(q, s, t, XH, XL, stop=False, chunk=chunk)
                        if t == 0:
                            if not first:
                                turn_out(q - 2, qb)
                            pe.wait_ge(c2_in[s], cb + 16)
                            hold(pe)
                        pe.matmul(PJ[q % 4][:], BC[s][:, 0:P], H2[:, t * NT:(t + 1) * NT], start=False, stop=True
                                  ).then_inc(prod, 1)

                def b_bases(i):
                    return (pe.snap(t_base + i * 2), [pe.snap(r_base[s] + i * 16) for s in range(2)],
                            pe.snap(q_base + i * 8), pe.snap(hf * (8 * KC) + i * 16))

                bases = b_bases(0)
                for s in range(2):
                    ffn_block(s, *bases, first=(s == 0))
                with pe.Fori(1, KC // 2 - 1) as i:
                    bases = b_bases(i)
                    for s in range(2):
                        ffn_block(s, *bases)
                bases = b_bases(KC // 2 - 1)
                for s in range(2):
                    ffn_block(s, *bases, last=(s == 1))
                turn_out(Q_O + 4 * KC - 2, q_base)

        @block.scalar
        def _(act):
            act.sem_inc(tb_taken, 1)
            def wf_hi(b):
                act.wait_ge(fold_turned, b + 2)
                act.copy(view(XH[:], KC, b * P, (b + 1) * P), view(TP[(b + 1) % 2][:], KC)).then_inc(fold_hi, 1)

            def w2_hi(i):
                act.wait_ge(fold_in[i % 2], 16 * (i // 2 + 1) if i < KC else 16 * (KC // 2 + KC))
                if i >= 2:
                    act.wait_ge(fold_prod, 3 * (i - 1))
                act.copy(WH[i % 2][:], RAW[i % 2][:]).then_inc(fold_hi, 1)

            for b in range(KC // 2):
                wf_hi(b)
            w2_hi(0)
            for b in range(KC // 2, KC):
                wf_hi(b)
            w2_hi(1)
            for i in range(KC + 1):
                if i + 2 <= KC:
                    w2_hi(i + 2)
                act.wait_ge(fold_taken, 3 * (i + 1))
                rows = MT[:, (i % 4) * D:(i % 4 + 1) * D]
                if i < KC:
                    act.dma_start(m_d.rearrange("o p (k n) -> k p o n", k=KC)[i], view(rows, KC)
                                  ).then_inc(m_out[i % 4], 16)
                else:
                    act.dma_start(c2_d, rows).then_inc(m_out[i % 4], 16)
            act.wait_ge(const_in, 16 * 5)
            hold(act)

            with act.Fori(0, HALVES) as hf:
                q_base, t_base = per_half(act, hf)
                r_base = [act.snap(hf * RAW_GAIN[s]) for s in range(2)]

                def is_turned(k, base=None):
                    act.wait_ge(turned, (t_base if base is None else base) + (k + 1 + 2))

                def is_prod(q, base=None):
                    act.wait_ge(prod, (q_base if base is None else base) + (q + 1))

                def w_hi(par, s):
                    act.copy(WH[s][:], TP[par][:]).then_inc(hi_done, 1)

                is_turned(T_W0)
                w_hi(0, 0)
                with act.Fori(0, TB // 2) as i:
                    tb = act.snap(t_base + i * 2)
                    for s in range(2):
                        is_turned(T_X + s, tb)
                        act.copy(view(XH[:], KC)[:, :, bass.ds(i * (2 * P) + s * P, P)],
                                 view(TP[(T_X + s) % 2][:], KC)).then_inc(hi_done, 1)
                act.wait_ge(a_in, hf * (16 * TT * SPT) + 16 * TT * SPT)
                act.copy(AH[:], AW[:]).then_inc(hi_done, 1)

                def wd(j, used, rg):
                    act.wait_ge(raw_in[j % 2], rg[j % 2] + raw_count(RAW_D + j))
                    act.wait_ge(prod, used)
                    act.copy(WH[j % 2][:], RAW[j % 2][:]).then_inc(wd_hi, 1)

                def b1_cols(s, j):
                    act.copy(view(BC[s][:], TT), view(B1S[:], TT)[:, :, bass.ds(j, P)]).then_inc(bc_in, 1)

                def w1_block(s, i, tb, qb, first=False, last=False):
                    if last:
                        wd(0, q_base + (Q_G - 2), r_base)
                    else:
                        is_turned(T_W + s + 1, tb)
                        if not first:
                            act.wait_ge(prod, qb + (Q_C + 2 * s))
                        w_hi(1 - s, 1 - s)
                        b1_cols(1 - s, i * (2 * P) + (s + 1) * P)
                    for t in range(TT):
                        is_prod(Q_C + 2 * s + t, qb)
                        act.activation(CH[:, bass.ds(i * (2 * TOK) + s * TOK + t * NT, NT)], PJ[(Q_C + 2 * s + t) % 4][:],
                                       ACT.Identity, bias=B1C[:, bass.ds(i * 2 + s, 1)]).then_inc(hi_done, 1)

                act.wait_ge(b1_in, hf * (16 * TT * SPT) + 16 * TT * SPT)
                b1_cols(0, 0)
                bases = act.snap(t_base), act.snap(q_base)
                for s in range(2):
                    w1_block(s, 0, *bases, first=(s == 0))
                with act.Fori(1, KC // 2 - 1) as i:
                    bases = act.snap(t_base + i * 2), act.snap(q_base + i * 4)
                    for s in range(2):
                        w1_block(s, i, *bases)
                i = KC // 2 - 1
                bases = act.snap(t_base + i * 2), act.snap(q_base + i * 4)
                for s in range(2):
                    w1_block(s, i, *bases, last=(s == 1))

                def group(g, last=False):
                    qg = act.snap(q_base + g * Q_PER_G)
                    rg = [act.snap(r_base[s] + g * (8 * PER_G)) for s in range(2)]
                    ug = act.snap(hf * (NKV * 8) + g * 8)
                    kg = act.snap(hf * (NKV * 10) + g * 10)

                    def take_v(t):
                        act.wait_ge(tb_done, kg + (t + 1))
                        act.copy(V[:, t * BPT * HD:(t + 1) * BPT * HD], TBK).then_inc(tb_taken, 1)

                    def attention(j):
                        if 0 <= j - 6 < 8:
                            u = j - 6
                            act.wait_ge(tb_done, kg + (TT + u + 1))
                            if u >= 2:
                                act.wait_ge(pv_done, ug + (u - 1))
                            act.copy(PT[:, (u % 2) * NT:(u % 2 + 1) * NT], TBK).then_inc(tb_taken, 1)
                        if 0 <= j - 7 < 8:
                            u = j - 7
                            act.wait_ge(pv_done, ug + (u + 1))
                            c = (u // 2) * TOK + (u % 2) * NT
                            act.copy(OH[:, c:c + NT], OB).then_inc(hi_done, 1)
                        if 0 <= j - 5 < 8:
                            u = j - 5
                            act.wait_ge(nmax_in, ug + (u + 1))
                            for b in range(BPT):
                                c, r = (u % 2) * NT + b * P, (u % 2) * BPT + b
                                ins = act.activation(SM[:, c:c + P], SM[:, c:c + P], ACT.Exp, bias=NMX[:, r:r + 1],
                                                     scale=SM_SCALE, accum_out=SUM[:, r:r + 1])
                            ins.then_inc(exp_in, 1)

                    def weights(j, used):
                        wd(j, qg + (Q_G + used), rg)

                    weights(1, 0)
                    weights(2, 2)
                    take_v(0)
                    weights(3, 4)
                    take_v(1)
                    attention(5)
                    weights(4, 6)
                    attention(6)
                    attention(7)
                    weights(5, 8)
                    attention(8)
                    attention(9)
                    weights(6, 10)
                    attention(10)
                    attention(11)
                    weights(7, 12)
                    attention(12)
                    attention(13)
                    weights(8, 20)
                    attention(14)
                    weights(9, 28)
                    if not last:
                        wd(0, qg + (Q_G + 36), [r + 8 * PER_G for r in rg])

                with act.Fori(0, NKV - 1) as g:
                    group(g)
                group(NKV - 1, last=True)

                act.wait_ge(prod, q_base + (Q_3 - 8))
                act.copy(view(WH[0][:], KC, 0, M_AR), view(AR32[:], KC)).then_inc(wd_hi, 1)
                for k in range(KC):
                    for t in range(TT):
                        act.wait_ge(taken, q_base + (Q_3 - 16 + 2 * k + t + 1 + 4))
                        xs = slice(k * TOK + t * NT, k * TOK + (t + 1) * NT)
                        act.copy(CH[:, xs], X1[:, xs]).then_inc(hi_done, 1)
                is_turned(T_A2)
                w_hi(T_A2 % 2, 1)

                def m_hi(j, used):
                    r = RAW_M + j
                    act.wait_ge(raw_in[r % 2], r_base[r % 2] + raw_count(r))
                    is_prod(Q3[used])
                    act.copy(WH[j % 2][:], RAW[r % 2][:]).then_inc(hi_done, 1)

                def g_hi(c):
                    act.wait_ge(g_prod, hf * KC + (c + 1))
                    act.copy(XH[:, c * TOK:(c + 1) * TOK], G32[:, c * TOK:(c + 1) * TOK]).then_inc(hi_done, 1)

                m_hi(0, "ar1")
                act.wait_ge(logits_in, hf * 2 + 1)
                act.activation(SC[:, TB:2 * TB], SC[:, 0:TB], ACT.Exp).then_inc(rexp, 1)
                m_hi(1, "h1")
                m_hi(2, "m01")
                m_hi(3, "m11")
                act.wait_ge(taken, q_base + (Q3["bh1"] + 1 + 4))
                for half in range(2):
                    ins = act.copy(HF[half * RF:(half + 1) * RF, :], AF32[0:RF, :])
                ins.then_inc(hf_in, 1)
                act.wait_ge(logits_in, hf * 2 + 2)
                act.activation(PR[:], PR[:], ACT.Exp).then_inc(rexp, 1)
                m_hi(4, "m21")
                m_hi(5, "m31")
                m_hi(6, "m41")
                for c in range(3):
                    g_hi(c)
                m_hi(7, "m51")
                for c in range(3, 7):
                    g_hi(c)
                is_turned(T_B)
                is_prod(Q3["m61"])
                w_hi(T_B % 2, 0)
                g_hi(7)

                def store(o, q, qb):
                    for t in range(TT):
                        act.wait_ge(taken, qb + (q + t + 1 + 4))
                        act.dma_start(out[bass.ds(hf * TOK + t * NT, NT), bass.ds(o, P)]
                                      .rearrange("(b p) n -> p b n", p=P),
                                      view(OS[t][:], BPT)).then_inc(out_done[t], 16)

                def ffn_block(s, o, tb, qb, first=False, last=False):
                    if not last:
                        is_turned(T_B + s + 1, tb)
                        act.wait_ge(prod, qb + (Q_O if first else Q_O + 4 * (s - 1) + 2))
                        w_hi((T_B + s + 1) % 2, 1 - s)
                    if not first:
                        store(o - P, Q_O + 4 * s - 2, qb)

                bases = act.snap(t_base), act.snap(q_base)
                for s in range(2):
                    ffn_block(s, s * P, *bases, first=(s == 0))
                with act.Fori(1, KC // 2 - 1) as i:
                    bases = act.snap(t_base + i * 2), act.snap(q_base + i * 8)
                    for s in range(2):
                        ffn_block(s, i * (2 * P) + s * P, *bases)
                i = KC // 2 - 1
                bases = act.snap(t_base + i * 2), act.snap(q_base + i * 8)
                for s in range(2):
                    ffn_block(s, i * (2 * P) + s * P, *bases, last=(s == 1))
                store(D - P, Q_O + 4 * KC - 2, q_base)

        @block.gpsimd
        def _(pool):
            pool.sem_inc(split_d, 2)
            with pool.Fori(0, HALVES) as hf:
                q_base, t_base = per_half(pool, hf)
                with pool.Fori(0, TB) as i:
                    pool.wait_ge(split_t, t_base + i + (T_X + 1 + 2))
                    hold(pool)
                    xs = bass.ds(i * P, P)
                    pool.tensor_tensor(view(X1[:], KC)[:, :, xs], view(XH[:].bitcast(F32), KC)[:, :, xs],
                                       view(XL[:].bitcast(F32), KC)[:, :, xs], ALU.add).then_inc(x_res, 1)
                with pool.Fori(0, NKV) as g:
                    dg = pool.snap(hf * SPLIT_D + g * PER_G)
                    for j in range(PER_G):
                        pool.wait_ge(wd_hi, dg + (j + 1))
                        hold(pool)
                        pool.tensor_tensor(WL[j % 2][:], RAW[j % 2][:], WH[j % 2][:].bitcast(F32), ALU.subtract
                                           ).then_inc(split_d, 1)
                pool.wait_ge(wd_hi, hf * SPLIT_D + SPLIT_D)
                hold(pool)
                pool.tensor_tensor(view(WL[0][:], KC, 0, M_AR), view(AR32[:], KC),
                                   view(WH[0][:].bitcast(F32), KC, 0, M_AR), ALU.subtract).then_inc(split_d, 1)

                pool.wait_ge(hf_in, hf + 1)
                hold(pool)
                for c in range(KC):
                    cs = slice(c * TOK, (c + 1) * TOK)
                    pool.wait_ge(comb_in[c // 2], hf * 64 + 64)
                    hold(pool)
                    pool.tensor_tensor(G32[:, cs], G32[:, cs], HF[:], ALU.mult).then_inc(g_prod, 1)

        @block.vector
        def _(dve):
            dve.sem_inc(taken, 4)
            dve.sem_inc(split_t, 2)
            dve.sem_inc(s_masked, 2)
            dve.sem_inc(o_split, 1)

            def wf_lo(b):
                dve.wait_ge(fold_hi, b + 1 + (b >= KC // 2))
                dve.tensor_tensor(view(XL[:], KC, b * P, (b + 1) * P), view(TP[(b + 1) % 2][:], KC),
                                  view(XH[:].bitcast(F32), KC, b * P, (b + 1) * P), ALU.subtract
                                  ).then_inc(fold_split, 1)

            def w2_lo(i):
                dve.wait_ge(fold_hi, KC // 2 + 1 if i == 0 else KC + 1 + i)
                dve.tensor_tensor(WL[i % 2][:], RAW[i % 2][:], WH[i % 2][:].bitcast(F32), ALU.subtract
                                  ).then_inc(fold_w, 1)

            def take(i, n):
                q = 3 * i + n
                dve.wait_ge(fold_prod, q + 1)
                if n == 0:
                    dst = AR32[:, i * M_AR:i * M_AR + M_AF] if i < KC else BA32[:]
                    ins = dve.tensor_copy(dst, PJ[q % 4][:, 0:M_AF])
                else:
                    if i >= 4:
                        dve.wait_ge(m_out[i % 4], 16 * (i // 4))
                    c = (i % 4) * D + (n - 1) * NT
                    ins = dve.tensor_copy(MT[:, c:c + NT], PJ[q % 4][:])
                ins.then_inc(fold_taken, 1)

            dve.wait_ge(fold_turned, 1)
            dve.tensor_copy(view(AR32[:], KC, M_AF, M_AR), view(TP[0][:], KC, M_AF, M_AR))
            dve.tensor_copy(view(ES[:], KC), view(TP[0][:], KC, 0, M_AF)).then_inc(fold_split, 1)
            for b in range(KC // 2):
                wf_lo(b)
            w2_lo(0)
            steps = [0]

            def chain(base, ins):
                ins.then_inc(step, 1)
                steps[0] += 1
                dve.wait_ge(step, base + steps[0])

            take(0, 0)
            for b in range(KC // 2, KC):
                wf_lo(b)
            w2_lo(1)
            take(0, 1)
            take(0, 2)
            dve.wait_ge(const_in, 16 * 5)
            n = HALVES * TB
            chain(0, dve.tensor_copy(LIDF[:], LID[:]))
            lb3 = view(LB[:], n)
            chain(0, dve.tensor_tensor(lb3, iota[:, 0:E2].unsqueeze(1).to_broadcast([P, n, E2]),
                                       LIDF[:].unsqueeze(2).to_broadcast([P, n, E2]), ALU.is_equal))
            chain(0, dve.tensor_scalar(LB[:], LB[:], LANG_BIAS, None, ALU.mult))

            for i in range(1, KC + 1):
                if i < KC:
                    w2_lo(i + 1)
                for n in range(3):
                    take(i, n)
            with dve.Fori(0, HALVES) as hf:
                q_base, t_base = per_half(dve, hf)
                h_base = dve.snap(hf * HI_N)
                s_base = dve.snap(hf * STEP_N + 3)
                steps[0] = 0

                def hi_is(n, base=None):
                    dve.wait_ge(hi_done, (h_base if base is None else base) + (n + 1))

                def is_prod(q, base=None):
                    dve.wait_ge(prod, (q_base if base is None else base) + (q + 1))

                def w_lo(par, s):
                    dve.tensor_tensor(WL[s][:], TP[par][:], WH[s][:].bitcast(F32), ALU.subtract).then_inc(split_t, 1)

                hi_is(H_W)
                w_lo(0, 0)
                with dve.Fori(0, TB // 2) as i:
                    hb = dve.snap(h_base + i * 2)
                    for s in range(2):
                        hi_is(H_X + s, hb)
                        xs = bass.ds(i * (2 * P) + s * P, P)
                        dve.tensor_tensor(view(XL[:], KC)[:, :, xs], view(TP[(T_X + s) % 2][:], KC),
                                          view(XH[:].bitcast(F32), KC)[:, :, xs], ALU.subtract).then_inc(split_t, 1)
                hi_is(H_A)
                dve.tensor_tensor(AL[:], AW[:], AH[:].bitcast(F32), ALU.subtract).then_inc(a_split, 1)

                def w1_block(s, i, hb, qb, first=False, last=False):
                    if first:
                        for t in range(TT):
                            is_prod(Q_H + t)
                            dve.tensor_tensor(view(HM[:, t * NT:(t + 1) * NT], SPT), view(PJ[(Q_H + t) % 4][:], SPT),
                                              CT[:, C_LORA:C_LORA + SPT].unsqueeze(2).to_broadcast([P, SPT, SEQ]),
                                              ALU.mult).then_inc(taken, 1)
                        for r in range(4):
                            dve.wait_ge(m_out[r], 16 * (KC // 4 + (r == 0)))
                        hold(dve)
                    n = H_C + 3 * s
                    if not last:
                        hi_is(n, hb)
                        w_lo(1 - s, 1 - s)
                        n += 1
                    for t in range(TT):
                        hi_is(n + t, hb)
                        cs = bass.ds(i * (2 * TOK) + s * TOK + t * NT, NT)
                        dve.scalar_tensor_tensor(out=CL[:, cs], in0=PJ[(Q_C + 2 * s + t) % 4][:],
                                                 scalar=B1C[:, bass.ds(i * 2 + s, 1)], in1=CH[:].bitcast(F32)[:, cs],
                                                 op0=ALU.add, op1=ALU.subtract).then_inc(taken, 1)

                bases = dve.snap(h_base), dve.snap(q_base)
                for s in range(2):
                    w1_block(s, 0, *bases, first=(s == 0))
                with dve.Fori(1, KC // 2 - 1) as i:
                    bases = dve.snap(h_base + i * 6), dve.snap(q_base + i * 4)
                    for s in range(2):
                        w1_block(s, i, *bases)
                i = KC // 2 - 1
                bases = dve.snap(h_base + i * 6), dve.snap(q_base + i * 4)
                for s in range(2):
                    w1_block(s, i, *bases, last=(s == 1))

                dve.wait_ge(x_res, hf * TB + TB)
                hold(dve)
                with dve.Fori(0, NKV) as g:
                    qg = dve.snap(q_base + g * Q_PER_G)
                    hg = dve.snap(h_base + g * 8)
                    ug = dve.snap(hf * (NKV * 8) + g * 8)
                    kg = dve.snap(hf * (NKV * 10) + g * 10)
                    cos = CT[:, C_COS:C_COS + SEQ].unsqueeze(1).to_broadcast([P, SPT, SEQ])
                    hd2 = HD // 2

                    def rotate(j, dst):
                        is_prod(Q_G + j, qg)
                        src = view(PJ[(Q_G + j) % 4][:], SPT)
                        rs = slice((j % 2) * NT, (j % 2 + 1) * NT)
                        dve.tensor_tensor(view(RC[:, rs], SPT), src, cos, ALU.mult)
                        for a, b in ((0, hd2), (hd2, 0)):
                            sin = CT[b:b + hd2, C_SIN:C_SIN + SEQ].unsqueeze(1).to_broadcast([hd2, SPT, SEQ])
                            ins = dve.tensor_tensor(view(RS[a:a + hd2, rs], SPT), src[b:b + hd2], sin, ALU.mult)
                        ins.then_inc(taken, 1)
                        dve.wait_ge(taken, qg + (Q_G + j + 1 + 4))
                        dve.tensor_tensor(dst, RC[:, rs], RS[:, rs], ALU.add).then_inc(qk_in, 1)

                    def mask_and_max(u):
                        us, ms = slice((u % 2) * NT, (u % 2 + 1) * NT), slice((u % 2) * BPT, (u % 2 + 1) * BPT)
                        dve.wait_ge(scores, ug + (u + 1))
                        mask = CT[:, C_MASK:C_MASK + P].unsqueeze(1).to_broadcast([P, BPT, P])
                        dve.tensor_tensor(view(SM[:, us], BPT), view(SB_[u % 2], BPT), mask, ALU.add
                                          ).then_inc(s_masked, 1)
                        dve.wait_ge(s_masked, ug + (u + 1 + 2))
                        dve.tensor_reduce(MX[:, ms], view(SM[:, us], BPT), AX.X, ALU.max).then_inc(max_in, 1)
                        dve.wait_ge(max_in, ug + (u + 1))
                        dve.tensor_scalar(NMX[:, ms], MX[:, ms], -SM_SCALE, None, ALU.mult).then_inc(nmax_in, 1)

                    def normalise(u):
                        us, ms = slice((u % 2) * NT, (u % 2 + 1) * NT), slice((u % 2) * BPT, (u % 2 + 1) * BPT)
                        dve.wait_ge(exp_in, ug + (u + 1))
                        dve.reciprocal(RCP[:, ms], SUM[:, ms]).then_inc(rcp_in, 1)
                        dve.wait_ge(rcp_in, ug + (u + 1))
                        dve.tensor_tensor(view(SM[:, us], BPT), view(SM[:, us], BPT),
                                          RCP[:, ms].unsqueeze(2).to_broadcast([P, BPT, P]), ALU.mult
                                          ).then_inc(probs_in, 1)

                    def split_o(u):
                        hi_is(H_G + u, hg)
                        c = (u // 2) * TOK + (u % 2) * NT
                        dve.tensor_tensor(OL[:, c:c + NT], OB, OH[:].bitcast(F32)[:, c:c + NT], ALU.subtract
                                          ).then_inc(o_split, 1)

                    for j in range(12):
                        if j >= 6:
                            normalise(j - 6)
                        if j >= 8:
                            split_o(j - 8)
                        if j < 2:
                            rotate(j, K[:, j * NT:(j + 1) * NT])
                        elif j < 4:
                            is_prod(Q_G + j, qg)
                            if j == TT + 1:
                                dve.wait_ge(tb_done, kg + 1)
                            dve.tensor_copy(VT[:], PJ[(Q_G + j) % 4][:]).then_inc(taken, 1)
                        else:
                            u = j - 4
                            rotate(j, Q[:, (u % 2) * NT:(u % 2 + 1) * NT])
                        if j >= 5:
                            mask_and_max(j - 5)
                    after = {3: [(mask_and_max, 7)], 5: [(normalise, 7), (split_o, 5)], 9: [(split_o, 6)],
                             13: [(split_o, 7)]}
                    normalise(6)
                    split_o(4)
                    for i in range(32):
                        hh, oc, o4, t = i // 16, i // 8 % 2, i // 2 % 4, i % 2
                        q = Q_G + 12 + i
                        is_prod(q, qg)
                        if i % 16 == 0:
                            dve.wait_ge(taken, qg + (q + 4))
                        xs = slice((oc * 4 + o4) * TOK + t * NT, (oc * 4 + o4) * TOK + (t + 1) * NT)
                        dve.tensor_tensor(X1[:, xs], PJ[q % 4][:], X1[:, xs], ALU.add).then_inc(taken, 1)
                        for f, u in after.get(i, ()):
                            f(u)

                dve.wait_ge(taken, q_base + (Q_3 + 4))
                for t in range(TT):
                    for k in range(KC):
                        xs = slice(k * TOK + t * NT, k * TOK + (t + 1) * NT)
                        hi_is(H_X1 + 2 * k + t)
                        dve.tensor_tensor(CL[:, xs], X1[:, xs], CH[:].bitcast(F32)[:, xs], ALU.subtract
                                          ).then_inc(x1_lo, 1)
                hi_is(H3["a2"])
                w_lo(T_A2 % 2, 1)

                def m_lo(j):
                    r = (RAW_M + j) % 2
                    hi_is(H3[f"m{j}"])
                    dve.tensor_tensor(WL[j % 2][:], RAW[r][:], WH[j % 2][:].bitcast(F32), ALU.subtract
                                      ).then_inc(split_m, 1)

                def m_take(j, t):
                    q = Q3[f"m{j}{t}"]
                    is_prod(q)
                    xs = slice(j * TOK + t * NT, j * TOK + (t + 1) * NT)
                    dve.scalar_tensor_tensor(out=X1[:, xs], in0=PJ[q % 4][:], scalar=BFC[:, j:j + 1], in1=X1[:, xs],
                                             op0=ALU.add, op1=ALU.add).then_inc(taken, 1)

                def g_lo(c):
                    hi_is(H3[f"g{c}"])
                    cs = slice(c * TOK, (c + 1) * TOK)
                    dve.tensor_tensor(XL[:, cs], G32[:, cs], XH[:].bitcast(F32)[:, cs], ALU.subtract
                                      ).then_inc(g_split, 1)

                def h2_take(t):
                    q = Q3[f"h{t}"]
                    is_prod(q)
                    dve.tensor_copy(H2[:, t * NT:(t + 1) * NT], PJ[q % 4][:]).then_inc(taken, 1)

                def take_gates(name, e):
                    for t in range(TT):
                        q = Q3[f"{name}{t}"]
                        is_prod(q)
                        dve.tensor_copy(GT[0:e, t * NT:(t + 1) * NT], PJ[q % 4][0:e, :]).then_inc(taken, 1)

                for t in range(TT):
                    q = Q3[f"ar{t}"]
                    is_prod(q)
                    dve.tensor_copy(AF32[0:M_AR, t * NT:(t + 1) * NT], PJ[q % 4][0:M_AR, :]).then_inc(taken, 1)
                h2_take(0)
                m_lo(0)
                for t in range(TT):
                    q = Q3[f"lt{t}"]
                    is_prod(q)
                    c = BPT * E2
                    dve.tensor_tensor(view(LG[:, t * c:(t + 1) * c], BPT),
                                      view(PJ[q % 4][:, 0:BPT * M_AR], BPT, M_AF, M_AR),
                                      view(LB[:, bass.ds(hf * (TT * c) + t * c, c)], BPT), ALU.add).then_inc(taken, 1)
                dve.wait_ge(taken, q_base + (Q3["lt1"] + 1 + 4))

                def sc(i):
                    return SC[:, i * TB:(i + 1) * TB]

                def top8(src, e):
                    hold(dve)
                    for b in range(TB):
                        ins = dve.max(M8[:, b * 8:(b + 1) * 8], src[:, b * e:(b + 1) * e])
                    chain(s_base, ins)

                def top8_index(src, e):
                    hold(dve)
                    for b in range(TB):
                        ins = dve.max_index(I8[:, b * 8:(b + 1) * 8], M8[:, b * 8:(b + 1) * 8],
                                            src[:, b * e:(b + 1) * e])
                    chain(s_base, ins)
                    chain(s_base, dve.tensor_copy(I8F[:], I8[:]))

                m8 = view(M8[:], TB)
                best = [m8[:, :, i] for i in range(2)]

                def gates(e):
                    i3 = iota[:, 0:e].unsqueeze(1).to_broadcast([P, TB, e])
                    ga, pr = view(GA[:, 0:TB * e], TB), view(PR[:, 0:TB * e], TB)
                    for i, dst in enumerate((ga, pr)):
                        idx = view(I8F[:], TB)[:, :, i:i + 1].to_broadcast([P, TB, e])
                        chain(s_base, dve.tensor_tensor(dst, i3, idx, ALU.is_equal))
                        chain(s_base, dve.tensor_tensor(dst, dst, sc(4 + i).unsqueeze(2).to_broadcast([P, TB, e]),
                                                        ALU.mult))
                    dve.tensor_tensor(ga, ga, pr, ALU.add).then_inc(gates_in_sb, 1)

                top8(LG, E2)
                top8_index(LG, E2)
                dve.tensor_tensor(sc(0), best[1], best[0], ALU.subtract).then_inc(logits_in, 1)
                dve.wait_ge(rexp, hf * 2 + 1)
                chain(s_base, dve.tensor_scalar(sc(2), sc(1), 1.0, None, ALU.add))
                chain(s_base, dve.reciprocal(sc(3), sc(2)))
                chain(s_base, dve.tensor_scalar(sc(4), sc(3), LORA_SCALE, None, ALU.mult))
                chain(s_base, dve.scalar_tensor_tensor(out=sc(5), in0=sc(1), scalar=LORA_SCALE, in1=sc(3),
                                                       op0=ALU.mult, op1=ALU.mult))
                gates(E2)
                h2_take(1)
                m_lo(1)
                m_take(0, 0)
                m_take(0, 1)
                m_lo(2)
                take_gates("gt", E2)
                m_take(1, 0)
                m_take(1, 1)
                dve.wait_ge(taken, q_base + (Q3["gt1"] + 1 + 4))
                dve.wait_ge(gates_in, hf * (16 * E2) + 16 * E2)
                dve.tensor_tensor(H2[:], H2[:], GT[:], ALU.mult).then_inc(hg_in, 1)
                m_lo(3)
                m_take(2, 0)
                for t in range(TT):
                    q = Q3[f"bh{t}"]
                    is_prod(q)
                    ts = slice(t * NT, (t + 1) * NT)
                    dve.tensor_tensor(AF32[0:M_AF, ts], PJ[q % 4][0:M_AF, :], AF32[0:M_AF, ts], ALU.add
                                      ).then_inc(taken, 1)
                m_take(2, 1)
                for t in range(TT):
                    q = Q3[f"lf{t}"]
                    is_prod(q)
                    dve.tensor_copy(view(LG[:, t * BPT * EF:(t + 1) * BPT * EF], BPT),
                                    view(PJ[q % 4][:, 0:BPT * M_AF], BPT, RF, M_AF)).then_inc(taken, 1)
                dve.wait_ge(taken, q_base + (Q3["lf1"] + 1 + 4))
                top8(LG, EF)
                pr3 = view(PR[:], TB)
                dve.tensor_tensor(pr3, view(LG[:], TB), m8[:, :, 0:1].to_broadcast([P, TB, EF]), ALU.subtract
                                  ).then_inc(logits_in, 1)
                dve.wait_ge(rexp, hf * 2 + 2)
                chain(s_base, dve.tensor_reduce(sc(0), pr3, AX.X, ALU.add))
                chain(s_base, dve.reciprocal(sc(1), sc(0)))
                chain(s_base, dve.tensor_tensor(pr3, pr3, sc(1).unsqueeze(2).to_broadcast([P, TB, EF]), ALU.mult))
                top8(PR, EF)
                top8_index(PR, EF)
                chain(s_base, dve.tensor_tensor(sc(2), best[0], best[1], ALU.add))
                chain(s_base, dve.tensor_scalar(sc(2), sc(2), 1e-6, None, ALU.add))
                chain(s_base, dve.reciprocal(sc(3), sc(2)))
                for i in range(2):
                    chain(s_base, dve.scalar_tensor_tensor(out=sc(4 + i), in0=best[i], scalar=FFN_SCALE, in1=sc(3),
                                                           op0=ALU.mult, op1=ALU.mult))
                gates(EF)
                m_lo(4)
                m_take(3, 0)
                m_take(3, 1)
                take_gates("gf", EF)
                m_lo(5)
                m_take(4, 0)
                m_take(4, 1)
                m_lo(6)
                g_lo(0)
                g_lo(1)
                m_take(5, 0)
                g_lo(2)
                m_take(5, 1)
                m_lo(7)
                g_lo(3)
                g_lo(4)
                m_take(6, 0)
                g_lo(5)
                g_lo(6)
                m_take(6, 1)
                hi_is(H3["b0"])
                w_lo(T_B % 2, 0)
                g_lo(7)
                m_take(7, 0)
                m_take(7, 1)

                dve.wait_ge(taken, q_base + (Q_O + 4))

                def ffn_block(s, o, hb, qb, first=False, last=False):
                    if not last:
                        hi_is(H_B + s, hb)
                        w_lo((T_B + s + 1) % 2, 1 - s)
                    if not first:
                        take_out(o, Q_O + 4 * s - 2, qb)
                    for t in range(TT):
                        q = Q_O + 4 * s + t
                        is_prod(q, qb)
                        dve.tensor_tensor(OT[t][:], PJ[q % 4][:], X1[:, bass.ds(o * TOK + t * NT, NT)], ALU.add
                                          ).then_inc(taken, 1)

                def take_out(o, q, qb):
                    for t in range(TT):
                        is_prod(q + t, qb)
                        dve.wait_ge(out_done[t], (hf * KC + o) * 16)
                        dve.tensor_copy(OS[t][:], PJ[(q + t) % 4][:]).then_inc(taken, 1)

                bases = dve.snap(h_base), dve.snap(q_base)
                for s in range(2):
                    ffn_block(s, s, *bases, first=(s == 0))
                with dve.Fori(1, KC // 2 - 1) as i:
                    bases = dve.snap(h_base + i * 2), dve.snap(q_base + i * 8)
                    for s in range(2):
                        ffn_block(s, i * 2 + s, *bases)
                i = KC // 2 - 1
                bases = dve.snap(h_base + i * 2), dve.snap(q_base + i * 8)
                for s in range(2):
                    ffn_block(s, i * 2 + s, *bases, last=(s == 1))
                take_out(KC, Q_O + 4 * KC - 2, q_base)
                assert steps[0] == STEP_N, steps[0]


def kernel(x, itok_B_0_23, itok_B_0_7, L0_cond_W, L0_cond_b, L0_cond_lora_As, L0_cond_lora_Bs, L0_attn_wq,
           L0_attn_wk, L0_attn_wv, L0_attn_wo, L0_cond2_W, L0_cond2_Wr, L0_cond2_A, L0_cond2_B, L0_ffn_base_w,
           L0_ffn_base_b, L0_ffn_A, L0_ffn_B, L0_ffn_router_w):
    import concourse.bacc as bacc
    from concourse.bass_utils import run_bass_kernel_spmd

    host = {
        "x": np.asarray(x).reshape(BATCH * SEQ, D),
        "ids1": np.asarray(itok_B_0_23),
        "ids2": np.asarray(itok_B_0_7).reshape(BATCH // 2, 2).T,
        "W1": np.asarray(L0_cond_W),
        "b1": np.asarray(L0_cond_b).reshape(KC, P).T,
        "A1": np.asarray(L0_cond_lora_As).reshape(SLOTS * D, RANK1),
        "B1": np.asarray(L0_cond_lora_Bs).reshape(SLOTS * RANK1, D),
        "wq": np.asarray(L0_attn_wq),
        "wk": np.asarray(L0_attn_wk),
        "wv": np.asarray(L0_attn_wv),
        "wo": np.asarray(L0_attn_wo),
        "W2": np.asarray(L0_cond2_W),
        "Wr2": np.asarray(L0_cond2_Wr),
        "A2": np.asarray(L0_cond2_A).reshape(E2 * R2, D),
        "B2": np.asarray(L0_cond2_B),
        "Wf": np.asarray(L0_ffn_base_w),
        "bf": np.asarray(L0_ffn_base_b).reshape(KC, P).T,
        "Af": np.asarray(L0_ffn_A),
        "Bf": np.asarray(L0_ffn_B),
        "Rf": np.asarray(L0_ffn_router_w),
        "consts": constants(),
    }
    nc = bacc.Bacc("TRN2", target_bir_lowering=False, num_devices=1)
    arrays, args = {}, {}
    for name, a in host.items():
        a = np.ascontiguousarray(a)
        arrays[f"in_{name}"] = a
        args[name] = nc.dram_tensor(f"in_{name}", a.shape, mybir.dt.from_np(a.dtype), kind="ExternalInput").ap()
    args["gates_d"] = nc.dram_tensor("gates_scratch", (E2 + EF, TOK), F32, kind="Internal").ap()
    args["m_d"] = nc.dram_tensor("m_scratch", (KC, P, D), F32, kind="Internal").ap()
    args["c2_d"] = nc.dram_tensor("c2_scratch", (P, D), F32, kind="Internal").ap()
    args["out"] = nc.dram_tensor("out_0", (BATCH * SEQ, D), F32, kind="ExternalOutput").ap()
    build(nc, **args)
    r = run_bass_kernel_spmd(nc, [arrays], core_ids=[0])
    return r.results[0]["out_0"].reshape(BATCH, SEQ, D)
```
